# Optimizing a Trainium2 kernel written in Bass

```python
import numpy as np
import jax
import jax.numpy as jnp

def _softmax(x, axis=-1):
    return jax.nn.softmax(x, axis=axis)

def _gelu(x):
    return jax.nn.gelu(x, approximate=True)

def _silu(x):
    return jax.nn.silu(x)

def _sigmoid(x):
    return jax.nn.sigmoid(x)

def _layernorm(x, axis=-1, eps=1e-05):
    m = jnp.mean(x, axis=axis, keepdims=True)
    v = jnp.var(x, axis=axis, keepdims=True)
    return (x - m) / jnp.sqrt(v + eps)

def _scatter_add(tgt, idx, src, axis=0):
    return tgt.at[idx].add(src)

def _segment_sum(src, seg, n):
    return jax.ops.segment_sum(src, seg, n)
kernel_name = 'mk_prb_d1_jaxref_r8_17d8d5'

def setup_inputs(seed: int=0):
    np.random.seed(seed)
    _w = jnp.asarray

    def _L0_attn_setup():
        import jax, jax.numpy as jnp
        import numpy as np
        D_MODEL = 128
        NUM_HEADS = 16
        D_HEAD = 64
        N_CTX = 256
        BATCH = 4
        NEG_INF = -10000000000.0
        key = jax.random.key(seed)
        k1, k2, k3, k4, k5 = jax.random.split(key, 5)
        s = 1.0 / np.sqrt(D_MODEL).astype(np.float32)
        x = jax.random.normal(k1, (BATCH, N_CTX, D_MODEL), dtype=jnp.float32)
        W_K = jax.random.normal(k2, (NUM_HEADS, D_HEAD, D_MODEL), dtype=jnp.float32) * s
        W_Q = jax.random.normal(k3, (NUM_HEADS, D_HEAD, D_MODEL), dtype=jnp.float32) * s
        W_V = jax.random.normal(k4, (NUM_HEADS, D_HEAD, D_MODEL), dtype=jnp.float32) * s
        W_O = jax.random.normal(k5, (D_MODEL, NUM_HEADS * D_HEAD), dtype=jnp.float32) * s
        return {'x': x, 'W_K': W_K, 'W_Q': W_Q, 'W_V': W_V, 'W_O': W_O}
    _L0_attn_in = _L0_attn_setup()

    def _L0_ffn_setup():
        import jax, jax.numpy as jnp
        import numpy as np
        NUM_EXPERTS_TOTAL = 9
        TOP_K = 2
        key = jax.random.key(seed)
        k0, k1, k2, k3, k4 = jax.random.split(key, 5)
        B, S, H, I = (2, 256, 128, 352)
        E = NUM_EXPERTS_TOTAL
        x = jax.random.normal(k0, (B, S, H), dtype=jnp.float32)
        Wr = jax.random.normal(k1, (H, E), dtype=jnp.float32) * 0.02
        Wg = jax.random.normal(k2, (E, H, I), dtype=jnp.float32) * 0.02
        Wu = jax.random.normal(k3, (E, H, I), dtype=jnp.float32) * 0.02
        Wd = jax.random.normal(k4, (E, I, H), dtype=jnp.float32) * 0.02
        return {'x': x, 'Wr': Wr, 'Wg': Wg, 'Wu': Wu, 'Wd': Wd}
    _L0_ffn_in = _L0_ffn_setup()
    _d = {'L0_attn_x': _L0_attn_in['x'], 'L0_attn_W_K': _L0_attn_in['W_K'], 'L0_attn_W_Q': _L0_attn_in['W_Q'], 'L0_attn_W_V': _L0_attn_in['W_V'], 'L0_attn_W_O': _L0_attn_in['W_O'], 'L0_ffn_Wr': _L0_ffn_in['Wr'], 'L0_ffn_Wg': _L0_ffn_in['Wg'], 'L0_ffn_Wu': _L0_ffn_in['Wu'], 'L0_ffn_Wd': _L0_ffn_in['Wd']}
    _x0 = _d['L0_attn_x']
    _d['L0_attn_x'] = jax.random.normal(jax.random.fold_in(jax.random.key(seed), 1), (2, 1024, 128), dtype=_x0.dtype)
    del _x0
    return _d

def reference(L0_attn_x, L0_attn_W_K, L0_attn_W_Q, L0_attn_W_V, L0_attn_W_O, L0_ffn_Wr, L0_ffn_Wg, L0_ffn_Wu, L0_ffn_Wd):

    def _L0_attn_ref(x, W_K, W_Q, W_V, W_O):
        import jax, jax.numpy as jnp
        import numpy as np
        D_MODEL = 128
        NUM_HEADS = 16
        D_HEAD = 64
        N_CTX = 256
        BATCH = 4
        NEG_INF = -10000000000.0
        b, q_len, d_model = x.shape
        d_head = W_K.shape[1]
        K = jnp.einsum('bpd,ihd->biph', x, W_K)
        Q = jnp.einsum('bpd,ihd->biph', x, W_Q)
        V = jnp.einsum('bpd,ihd->biph', x, W_V)
        scores = jnp.einsum('biph,biqh->biqp', K, Q)
        mask = jnp.tril(jnp.ones((q_len, q_len), dtype=bool))
        scores = jnp.where(mask[None, None, :, :], scores, NEG_INF)
        attn = jax.nn.softmax(scores / np.sqrt(d_head).astype(np.float32), axis=-1)
        z = jnp.einsum('biph,biqp->biqh', V, attn)
        z_flat = jnp.transpose(z, (0, 2, 1, 3)).reshape(b, q_len, -1)
        out = jnp.einsum('bqf,df->bqd', z_flat, W_O)
        return out

    def _L0_ffn_ref(x, Wr, Wg, Wu, Wd):
        import jax, jax.numpy as jnp
        import numpy as np
        NUM_EXPERTS_TOTAL = 9
        TOP_K = 2
        B, S, H = x.shape
        E = NUM_EXPERTS_TOTAL
        T = B * S
        logits = jnp.einsum('bsh,he->bse', x, Wr)
        probs = jax.nn.softmax(logits, axis=-1)
        topk_w, topk_idx = jax.lax.top_k(probs, TOP_K)
        topk_w = topk_w / jnp.sum(topk_w, axis=-1, keepdims=True)
        xf = x.reshape(T, H)
        wf = topk_w.reshape(T, TOP_K)
        idxf = topk_idx.reshape(T, TOP_K)
        cw = jnp.zeros((T, E), dtype=x.dtype).at[jnp.arange(T)[:, None], idxf].add(wf)
        gate = jax.nn.silu(jnp.einsum('th,ehi->tei', xf, Wg))
        hidden = gate * jnp.einsum('th,ehi->tei', xf, Wu)
        out = jnp.einsum('tei,eih,te->th', hidden, Wd, cw)
        return out.reshape(B, S, H)
    x = L0_attn_x
    xn = _layernorm(x, axis=-1)
    x = x + _L0_attn_ref(xn, L0_attn_W_K, L0_attn_W_Q, L0_attn_W_V, L0_attn_W_O) + _L0_ffn_ref(xn, L0_ffn_Wr, L0_ffn_Wg, L0_ffn_Wu, L0_ffn_Wd)
    return x

_drawn_inputs = setup_inputs


def setup_inputs(seed=0):
    import zlib

    import numpy as np

    out = dict(_drawn_inputs(seed))
    spreads = {}
    factors = {'L0_ffn_Wr': 8.0, 'L0_ffn_Wg': 8.0, 'L0_ffn_Wu': 8.0, 'L0_ffn_Wd': 8.0}
    for name, (base, spread) in spreads.items():
        noise = np.random.default_rng([zlib.crc32(name.encode()), seed]).standard_normal(out[name].shape)
        drawn = base * np.exp(spread * noise) if base else spread * noise
        out[name] = jnp.asarray(drawn.astype(out[name].dtype))
    for name, factor in factors.items():
        out[name] = (out[name] * factor).astype(out[name].dtype)
    return out
```

```python
from contextlib import ExitStack

import concourse.bass as bass
from concourse import mybir

ALU = mybir.AluOpType
ACT = mybir.ActivationFunctionType
AX_X = mybir.AxisListType.X
F32 = mybir.dt.float32
F32R = mybir.dt.float32r
BF16 = mybir.dt.bfloat16

P = 128
EPS = 1e-5
MASKED = -1e30


def bass_layernorm_causal_attention_plus_moe_kernel(
    nc: bass.Bass,
    x: bass.AP,
    W_K: bass.AP,
    W_Q: bass.AP,
    W_V: bass.AP,
    W_O: bass.AP,
    Wr: bass.AP,
    Wg: bass.AP,
    Wu: bass.AP,
    Wd: bass.AP,
    out: bass.AP,
):
    BATCH, S, D = x.shape
    HEADS, DH, _ = W_K.shape
    E, _, I = Wg.shape
    T = BATCH * S
    TT = T // P
    QT = S // P
    BLK = 512
    TB = T // BLK
    TPB = BLK // P
    QB = S // BLK
    PAIRS = HEADS // 2
    MT = -(-I // P)
    IP = MT * P
    ILAST = I - (MT - 1) * P
    assert D == P and 2 * DH == P and BATCH == 2 and S == 1024 and MT == 3 and E % 3 == 0

    x_tiles = x.rearrange("b (t p) d -> p (b t) d", p=P)
    out_tiles = out.rearrange("b (t p) d -> p (b t) d", p=P)
    w_pairs = [w.rearrange("(a two) h d -> a (two h) d", two=2) for w in (W_Q, W_K, W_V)]
    cw_dram = nc.dram_tensor("cw_dram", [E, T], F32).ap()

    def wait(eng, sem, value):
        if not isinstance(value, int) or value > 0:
            eng.wait_ge(sem, value)

    with ExitStack() as ctx:
        def sb(name, shape, dt=F32, stack=None):
            return (stack or ctx).enter_context(nc.sbuf_tensor(name, shape, dt))

        def psum(name, shape):
            return ctx.enter_context(nc.psum_tensor(name, shape, F32))

        def sem(name):
            return ctx.enter_context(nc.semaphore(name))

        ps_big = psum("ps_big", [P, 2, 2 * BLK])
        ps_mid = psum("ps_mid", [P, 2, BLK])
        ps_z = psum("ps_z", [P, BLK])
        ps_misc = psum("ps_misc", [P, BLK])

        x_tok = sb("x_tok", [P, TT, D])
        xT_hi = sb("xT_hi", [P, T], F32R)
        xT_lo = sb("xT_lo", [P, T], F32R)
        acc = sb("acc", [P, T])
        ident = sb("ident", [P, P])
        ident_bf = sb("ident_bf", [P, P], BF16)
        causal_bf = sb("causal_bf", [P, P], BF16)
        eps_col = sb("eps_col", [P, 1])
        raw_qkv = sb("raw_qkv", [P, 3, D])
        raw_o = sb("raw_o", [P, 2, 2, DH])

        moe = ExitStack()
        stats = sb("stats", [P, TT, 6], stack=moe)
        meanvar = sb("meanvar", [P, TT, 2], stack=moe)
        std = sb("std", [P, TT], stack=moe)
        rstd = sb("rstd", [P, TT], stack=moe)
        xn = sb("xn", [P, TT, D], stack=moe)
        xT = sb("xT", [P, T], stack=moe)
        wr_sb = sb("wr_sb", [P, E], stack=moe)
        rank = sb("rank", [P, TT, E], stack=moe)
        logit = sb("logit", [P, TT, E], stack=moe)
        prob = sb("prob", [P, TT, E], stack=moe)
        left = sb("left", [P, TT, E], stack=moe)
        pick = sb("pick", [P, 2, TT, E], stack=moe)
        vote = sb("vote", [P, TT, E], stack=moe)
        top = sb("top", [P, 4, TT], stack=moe)
        cw = sb("cw", [P, TT, E], stack=moe)
        cwT = sb("cwT", [E, T], stack=moe)
        raw_g = [sb(f"raw_g{j}", [P, I], stack=moe) for j in range(3)]
        raw_u = [sb(f"raw_u{j}", [P, I], stack=moe) for j in range(3)]
        raw_d = [sb(f"raw_d{j}", [P, MT, D], stack=moe) for j in range(3)]
        g_hi = [sb(f"g_hi{j}", [P, IP], F32R, moe) for j in range(3)]
        g_lo = [sb(f"g_lo{j}", [P, IP], F32R, moe) for j in range(3)]
        u_hi = [sb(f"u_hi{j}", [P, IP], F32R, moe) for j in range(3)]
        u_lo = [sb(f"u_lo{j}", [P, IP], F32R, moe) for j in range(3)]
        d_hi = [sb(f"d_hi{j}", [P, MT, D], F32R, moe) for j in range(3)]
        d_lo = [sb(f"d_lo{j}", [P, MT, D], F32R, moe) for j in range(3)]
        cw_bc = [sb(f"cw_bc{j}", [P, T], stack=moe) for j in range(3)]
        silu = [sb(f"silu{j}", [P, BLK], stack=moe) for j in range(2)]
        hid = [sb(f"hid{j}", [P, BLK], stack=moe) for j in range(2)]
        hid_hi = [sb(f"hid_hi{j}", [P, BLK], F32R, moe) for j in range(2)]
        hid_lo = [sb(f"hid_lo{j}", [P, BLK], F32R, moe) for j in range(2)]
        y_sc = [sb(f"y_sc{j}", [P, BLK], stack=moe) for j in range(2)]
        moe.close()

        w_hi = sb("w_hi", [P, 3, P], F32R)
        w_lo = sb("w_lo", [P, 3, P], F32R)
        wo_hi = sb("wo_hi", [P, 2, D], F32R)
        wo_lo = sb("wo_lo", [P, 2, D], F32R)
        q_parts = sb("q_parts", [P, 2, S], F32R)
        k_parts = sb("k_parts", [P, 2, S], F32R)
        vT = sb("vT", [P, S])
        q_st = [[sb(f"q_st{b}{h}", [P, S], F32R) for h in range(2)] for b in range(2)]
        k_st = [[sb(f"k_st{b}{h}", [P, 2, S], F32R) for h in range(2)] for b in range(2)]
        v_st = [sb(f"v_st{b}", [P, QT, 2, 2, DH], F32R) for b in range(2)]
        probs = [sb(f"probs{j}", [P, S]) for j in range(4)]
        pT_hi = [sb(f"pT_hi{j}", [P, TPB * (j + 1), BLK], F32R) for j in range(QB)]
        pT_lo = [sb(f"pT_lo{j}", [P, TPB * (j + 1), BLK], F32R) for j in range(QB)]
        z_hi = [[sb(f"z_hi{h}{j}", [P, BLK], F32R) for j in range(QB)] for h in range(2)]
        z_lo = [[sb(f"z_lo{h}{j}", [P, BLK], F32R) for j in range(QB)] for h in range(2)]
        neg_max = sb("neg_max", [P, 4 * QT])
        den = sb("den", [P, 4 * QT])
        rden = sb("rden", [P, 4 * QT])

        x_in = sem("x_in"); wr_in = sem("wr_in"); qkv_in = sem("qkv_in"); o_in = sem("o_in")
        raw_in = [sem(f"raw_in{j}") for j in range(3)]
        cw_in = [sem(f"cw_in{j}") for j in range(3)]
        cw_out = sem("cw_out"); out_sent = sem("out_sent")
        const_made = sem("const_made"); pool_order = sem("pool_order"); dve_order = sem("dve_order")
        var_done = sem("var_done"); std_done = sem("std_done"); xn_done = sem("xn_done")
        xT_ready = sem("xT_ready"); xT_copied = sem("xT_copied"); xhi_done = sem("xhi_done"); xlo_done = sem("xlo_done")
        logit_ready = sem("logit_ready"); shifted = sem("shifted"); exped = sem("exped")
        cw_done = sem("cw_done"); cwT_ready = sem("cwT_ready"); cwT_copied = sem("cwT_copied")
        whi_done = sem("whi_done"); wlo_done = sem("wlo_done")
        gate_ready = sem("gate_ready"); up_ready = sem("up_ready"); silu_done = sem("silu_done")
        hid_done = sem("hid_done"); hidhi_done = sem("hidhi_done"); hidlo_done = sem("hidlo_done")
        down_done = sem("down_done"); y_scaled = sem("y_scaled"); y_added = sem("y_added")
        pads_zero = sem("pads_zero")
        proj_filled = sem("proj_filled"); proj_copied = sem("proj_copied"); proj_split = sem("proj_split")
        stacked = sem("stacked")
        s_ready = sem("s_ready"); max_done = sem("max_done"); exp_done = sem("exp_done")
        rden_done = sem("rden_done"); normed = sem("normed")
        t_ready = sem("t_ready"); pT_copied = sem("pT_copied"); pT_split = sem("pT_split")
        z_ready = sem("z_ready"); z_copied = sem("z_copied"); z_split = sem("z_split")
        o_ready = sem("o_ready"); o_added = sem("o_added")
        acc_turned = sem("acc_turned"); out_made = sem("out_made")

        cwT_bank = [ps_mid[:, 0, :], ps_mid[:, 1, :], ps_z[:, :], ps_misc[:, :]]
        xT_bank = [ps_big[:, g // 2, (g % 2) * BLK:(g % 2 + 1) * BLK] for g in range(TB)]

        UPE = TB * MT
        UPI = 3 * UPE
        BPI = 3 * TB
        ITER = E // 3
        YBUF = 2
        DOWN_LAG = 2

        UPH = 2 * QT
        AHEAD = 3
        GROUPS = [t // TPB + 1 for t in range(QT)]
        GPH = sum(GROUPS)
        PROJ = ["q0", "q1", "k0", "k1", "v0", "v1", "t0", "t1", "wo",
                "wqkv", "q0", "q1", "k0", "k1", "v0", "v1", "t0", "t1"]
        PROJ_FIRST = PROJ[9:]
        PROJ_SLOT = {"wqkv": 1, "q0": 2, "q1": 3, "k0": 5, "k1": 6, "v0": 7, "v1": 9, "t0": 10, "t1": 11, "wo": 12}
        PV_SLOTS = [[(5, 0, 4)], [(8, 0, 3), (9, 3, 6), (10, 6, 8)]]
        OUT_SLOT = [UPH - 1, UPH + 4]
        SPLIT = [n for n in PROJ if n[0] != "v"]
        STACKS = 8

        def proj_count(p, k):
            return len(PROJ_FIRST) + len(PROJ) * p + k + 1

        def split_count(p, k):
            return 7 + len(SPLIT) * p + sum(n[0] != "v" for n in PROJ[:k + 1])

        def slot_plan(first, last):
            plan = {s: [] for s in range(-1, 3 * UPH)}
            for b in (-1, 0, 1):
                events = [(PROJ_SLOT[PROJ[k]], ("proj", k)) for k in range(9 * b, 9 * b + 9) if b >= 0 and not (last and b == 1)]
                for j in range(QB):
                    for h in range(2):
                        for at, k0, k1 in PV_SLOTS[j]:
                            events.append((h * QT + at, ("pv", (b, h, j, k0, k1))))
                        events.append((h * QT + at, ("z", (b, h, j))))
                    events.append((OUT_SLOT[j], ("o", (b, j))))
                for at, event in events:
                    if at + b * UPH >= -1 and not (b < 0 and first):
                        plan[at + b * UPH].append(event)
            return plan

        def z_count(p, b, h, j):
            return 8 * p + 4 * b + 2 * h + j + 1

        def o_count(p, b, j):
            return 4 * p + 2 * b + j + 1

        def unit_count(p, n):
            return 2 * UPH * p + n + 1

        def group_count(p, n):
            head, i = divmod(n, QT)
            return 4 * GPH * p + head * GPH + sum(GROUPS[:i + 1])

        def score_cols(i):
            width = (i + 1) * P
            off = P if width == BLK + P else 0
            end = max(off + width, 2 * P)
            parts = [(off, min(end, BLK))] + ([(BLK, end)] if end > BLK else [])
            return off, width, parts

        block = ctx.enter_context(nc.Block())

        @block.sync
        def _(sp):
            sp.dma_start(x_tok[:], x_tiles).then_inc(x_in, 16)
            sp.dma_start(wr_sb[:], Wr).then_inc(wr_in, 16)

            def load_expert(e, j):
                pick_e = (lambda w: w[e]) if isinstance(e, int) else (lambda w: w[bass.ds(e, 1)].rearrange("a r c -> (a r) c"))
                sp.dma_start(raw_g[j][:], pick_e(Wg)).then_inc(raw_in[j], 16)
                sp.dma_start(raw_u[j][:], pick_e(Wu)).then_inc(raw_in[j], 16)
                wd = pick_e(Wd)
                sp.dma_start(raw_d[j][:, 0:MT - 1, :], wd[0:(MT - 1) * P].rearrange("(m r) c -> r m c", r=P)).then_inc(raw_in[j], 16)
                sp.dma_start(raw_d[j][0:ILAST, MT - 1, :], wd[(MT - 1) * P:I]).then_inc(raw_in[j], 16)

            def load_cw(e, j):
                src = cw_dram[e:e + 1, :] if isinstance(e, int) else cw_dram[bass.ds(e, 1), :]
                sp.dma_start(cw_bc[j][:], src.broadcast_to([P, T])).then_inc(cw_in[j], 16)

            def load_qkv(p):
                for m, w in enumerate(w_pairs):
                    src = w[p] if isinstance(p, int) else w[bass.ds(p, 1)].rearrange("a r d -> (a r) d")
                    sp.dma_start(raw_qkv[:, m, :], src).then_inc(qkv_in, 16)

            def load_o(p):
                src = W_O[:, p * P:(p + 1) * P] if isinstance(p, int) else W_O[:, bass.ds(p * P, P)]
                for twice in range(2):
                    sp.dma_start(raw_o[:, :, twice, :], src.rearrange("d (h c) -> d h c", h=2)).then_inc(o_in, 16)

            def stack(p, b):
                k_q1, k_k1 = (1, 3) if b == 1 else (11, 13)
                before = p if b == 1 else p - 1
                wait(sp, proj_split, split_count(before, k_q1))
                for h in range(2):
                    rows = slice(DH * h, DH * (h + 1))
                    for part in range(2):
                        sp.dma_start(q_st[b][h][DH * part:DH * (part + 1), :].bitcast(F32),
                                     q_parts[rows, part, :].bitcast(F32)).then_inc(stacked, 16)
                wait(sp, proj_split, split_count(before, k_k1))
                for h in range(2):
                    rows = slice(DH * h, DH * (h + 1))
                    for copy in range(2):
                        sp.dma_start(k_st[b][h][DH * copy:DH * (copy + 1), :, :].bitcast(F32),
                                     k_parts[rows, :, :].bitcast(F32)).then_inc(stacked, 16)

            for e in range(3):
                load_expert(e, e)
            load_qkv(0)
            load_o(0)
            sp.wait_ge(cwT_copied, TB)
            sp.dma_start(cw_dram, cwT[:]).then_inc(cw_out, 16)
            sp.wait_ge(cw_out, 16)
            for e in range(3):
                load_cw(e, e)
            with sp.Fori(0, ITER - 1) as it:
                for j in range(3):
                    nxt = sp.snap(3 * it + j + 3)
                    sp.wait_ge(wlo_done, 3 * it + j + 1)
                    load_expert(nxt, j)
                    sp.wait_ge(y_scaled, YBUF + 12 * it + 4 * (j + 1))
                    load_cw(nxt, j)

            stack(0, 0)

            def iteration(p, last):
                if not last:
                    wait(sp, proj_filled, proj_count(p - 1, 9))
                    load_qkv(p + 1)
                stack(p, 1)
                if not last:
                    wait(sp, proj_filled, proj_count(p, 8))
                    load_o(p + 1)
                    stack(p + 1, 0)

            iteration(0, False)
            with sp.Fori(1, PAIRS - 1) as p:
                iteration(p, False)
            iteration(PAIRS - 1, True)
            for g in range(TB):
                sp.wait_ge(out_made, g + 1)
                sp.dma_start(out_tiles[:, g * TPB:(g + 1) * TPB, :], x_tok[:, g * TPB:(g + 1) * TPB, :]).then_inc(out_sent, 16)
            sp.wait_ge(out_sent, 16 * TB)

        @block.gpsimd
        def _(pool):
            pool.memset(ident[:], 0.0).then_inc(pool_order, 1)
            pool.memset(ident_bf[:], 0.0).then_inc(pool_order, 1)
            pool.memset(causal_bf[:], 0.0).then_inc(pool_order, 1)
            pool.memset(rank[:], 0.0).then_inc(pool_order, 1)
            pool.memset(eps_col[:], EPS).then_inc(const_made, 1)
            pool.wait_ge(pool_order, 4)
            pool.affine_select(out=ident[:], in_=ident[:], compare_op=ALU.not_equal, fill=1.0, base=0,
                               pattern=[[-1, P]], channel_multiplier=1).then_inc(const_made, 1)
            pool.affine_select(out=ident_bf[:], in_=ident_bf[:], compare_op=ALU.not_equal, fill=1.0, base=0,
                               pattern=[[-1, P]], channel_multiplier=1).then_inc(const_made, 1)
            pool.affine_select(out=causal_bf[:], in_=causal_bf[:], compare_op=ALU.is_ge, fill=MASKED, base=0,
                               pattern=[[-1, P]], channel_multiplier=1).then_inc(const_made, 1)
            for e in range(E):
                last = pool.memset(rank[:, :, e], float(E - e))
            last.then_inc(const_made, 1)
            for j in range(3):
                for w in (g_hi, g_lo, u_hi, u_lo):
                    pool.memset(w[j][:, I:IP].bitcast(F32), 0.0)
                for w in (d_hi, d_lo):
                    last = pool.memset(w[j][:, MT - 1, :].bitcast(F32), 0.0)
            last.then_inc(const_made, 1)
            pool.memset(acc[:], 0.0).then_inc(y_added, YBUF)

            def split_expert(e, j):
                pool.wait_ge(whi_done, 4 * e + 4)
                pool.tensor_tensor(g_lo[j][:, 0:I], raw_g[j][:], g_hi[j][:, 0:I].bitcast(F32), ALU.subtract)
                pool.tensor_tensor(u_lo[j][:, 0:I], raw_u[j][:], u_hi[j][:, 0:I].bitcast(F32), ALU.subtract)
                pool.tensor_tensor(d_lo[j][:, 0:MT - 1, :], raw_d[j][:, 0:MT - 1, :], d_hi[j][:, 0:MT - 1, :].bitcast(F32), ALU.subtract)
                pool.tensor_tensor(d_lo[j][0:ILAST, MT - 1, :], raw_d[j][0:ILAST, MT - 1, :],
                                   d_hi[j][0:ILAST, MT - 1, :].bitcast(F32), ALU.subtract).then_inc(wlo_done, 1)

            split_expert(0, 0)

            def experts(it, last):
                for k in range(BPI):
                    pool.wait_ge(y_scaled, YBUF + BPI * it + k + 1)
                    blk = slice((k % TB) * BLK, (k % TB + 1) * BLK)
                    pool.tensor_tensor(acc[:, blk], acc[:, blk], y_sc[k % YBUF][:], ALU.add).then_inc(y_added, 1)
                    if k % TB == 1 and not (last and k // TB == 2):
                        split_expert(3 * it + k // TB + 1, (k // TB + 1) % 3)

            with pool.Fori(0, ITER - 1) as it:
                experts(it, False)
            experts(ITER - 1, True)

            pool.wait_ge(y_added, YBUF + E * TB)
            for j in range(QB):
                for t in (pT_hi, pT_lo):
                    last = pool.memset(t[j][:, TPB * (j + 1) - 1, 2 * P:3 * P].bitcast(F32), 0.0)
            last.then_inc(pads_zero, 1)

            def norm(p, n):
                width = (n % QT + 1) * P
                rows = probs[n % 4][:, 0:width]
                col = rden[:, n:n + 1]
                pool.wait_ge(rden_done, unit_count(p, n))
                pool.tensor_tensor(rows, rows, col.to_broadcast([P, width]), ALU.mult).then_inc(normed, 1)

            norm(0, 0)

            def iteration(p, last):
                for s in range(2 * UPH):
                    n = s + AHEAD - 2
                    if n < 2 * UPH:
                        norm(p, n)
                    elif not last:
                        norm(p + 1, n - 2 * UPH)

            iteration(0, False)
            with pool.Fori(1, PAIRS - 1) as p:
                iteration(p, False)
            iteration(PAIRS - 1, True)

        @block.scalar
        def _(act):
            act.wait_ge(const_made, 6)
            act.wait_ge(var_done, 1)
            nc.scalar.activation(std[:], meanvar[:, :, 1], ACT.Sqrt, bias=eps_col[:]).then_inc(std_done, 1)
            for g in range(TB):
                act.wait_ge(xT_ready, g + 1)
                blk = slice(g * BLK, (g + 1) * BLK)
                nc.scalar.activation(xT[:, blk], xT_bank[g], ACT.Copy).then_inc(xT_copied, 1)
                nc.scalar.activation(xT_hi[:, blk], xT_bank[g], ACT.Copy).then_inc(xhi_done, 1)
            act.wait_ge(shifted, 1)
            nc.scalar.activation(prob[:], logit[:], ACT.Exp).then_inc(exped, 1)

            def split_expert(e, j, count):
                act.wait_ge(raw_in[j], 64 * count)
                nc.scalar.activation(g_hi[j][:, 0:I], raw_g[j][:], ACT.Copy).then_inc(whi_done, 1)
                nc.scalar.activation(u_hi[j][:, 0:I], raw_u[j][:], ACT.Copy).then_inc(whi_done, 1)
                nc.scalar.activation(d_hi[j][:, 0:MT - 1, :], raw_d[j][:, 0:MT - 1, :], ACT.Copy).then_inc(whi_done, 1)
                nc.scalar.activation(d_hi[j][0:ILAST, MT - 1, :], raw_d[j][0:ILAST, MT - 1, :], ACT.Copy).then_inc(whi_done, 1)

            split_expert(0, 0, 1)
            for g in range(TB):
                act.wait_ge(cwT_ready, g + 1)
                nc.scalar.activation(cwT[:, g * BLK:(g + 1) * BLK], cwT_bank[g][0:E, :], ACT.Copy).then_inc(cwT_copied, 1)

            def experts(it, last):
                for n in range(UPI + 1):
                    if n < UPI:
                        act.wait_ge(gate_ready, UPI * it + n + 1)
                        if n >= 2:
                            act.wait_ge(hid_done, UPI * it + n - 1)
                        nc.scalar.activation(silu[n % 2][:], ps_big[:, n % 2, 0:BLK], ACT.Silu).then_inc(silu_done, 1)
                    if n >= 1:
                        m = n - 1
                        act.wait_ge(hid_done, UPI * it + m + 1)
                        if m >= 2:
                            act.wait_ge(down_done, UPI * it + m - 1)
                        nc.scalar.activation(hid_hi[m % 2][:], hid[m % 2][:], ACT.Copy).then_inc(hidhi_done, 1)
                    if n % UPE == UPE // 2 and not (last and n // UPE == 2):
                        j = n // UPE
                        split_expert(3 * it + j + 1, (j + 1) % 3, it + 1 + (j + 1) // 3)

            with act.Fori(0, ITER - 1) as it:
                experts(it, False)
            experts(ITER - 1, True)

            def exp(p, n):
                off, width, _ = score_cols(n % QT)
                act.wait_ge(max_done, unit_count(p, n))
                if n >= 4:
                    act.wait_ge(t_ready, group_count(p, n - 4))
                else:
                    wait(act, t_ready, group_count(p - 1, n - 4 + 2 * UPH))
                nc.scalar.activation(probs[n % 4][:, 0:width], ps_big[:, n % 2, off:off + width], ACT.Exp,
                                     bias=neg_max[:, n:n + 1], accum_out=den[:, n:n + 1]).then_inc(exp_done, 1)

            def copy_probs(p, n):
                head, i = divmod(n, QT)
                j = i // TPB
                if i % TPB == 0:
                    wait(act, z_ready, z_count(p, head // 2, head % 2, j) - 2)
                for g in range(GROUPS[i]):
                    count = group_count(p, n) - GROUPS[i] + g + 1
                    tiles = min(TPB, i + 1 - g * TPB)
                    bank = (head * GPH + sum(GROUPS[:i]) + g) % 2
                    act.wait_ge(t_ready, count)
                    nc.scalar.activation(pT_hi[j][:, g * TPB:g * TPB + tiles, (i % TPB) * P:(i % TPB + 1) * P],
                                         ps_mid[:, bank, 0:tiles * P].rearrange("p (t q) -> p t q", t=tiles),
                                         ACT.Copy).then_inc(pT_copied, 1)

            def copy_proj(p, k, half, b_next):
                name = PROJ[k]
                act.wait_ge(proj_filled, proj_count(p, k))
                if name == "wqkv":
                    nc.scalar.activation(w_hi[:, 0, :], ps_misc[:, 0:P], ACT.Copy, scale=DH ** -0.5)
                    ins = nc.scalar.activation(w_hi[:, 1:3, :], ps_misc[:, P:3 * P].rearrange("p (m r) -> p m r", m=2), ACT.Copy)
                elif name == "wo":
                    ins = nc.scalar.activation(wo_hi[:], ps_misc[:, 0:2 * P].rearrange("p (h d) -> p h d", h=2), ACT.Copy)
                elif name[0] in "qk":
                    c = int(name[1])
                    if name == "q0":
                        wait(act, stacked, 16 * STACKS * half)
                    dst = q_parts if name[0] == "q" else k_parts
                    ins = nc.scalar.activation(dst[:, 0, c * BLK:(c + 1) * BLK], ps_misc[:, :], ACT.Copy)
                elif name[0] == "v":
                    c = int(name[1])
                    ins = nc.scalar.activation(vT[:, c * BLK:(c + 1) * BLK], ps_misc[:, :], ACT.Copy)
                else:
                    c = int(name[1])
                    ins = nc.scalar.activation(v_st[b_next][:, c * TPB:(c + 1) * TPB, :, 0, :],
                                               ps_misc[:, :].rearrange("p (t h c) -> p t h c", t=TPB, h=2), ACT.Copy)
                ins.then_inc(proj_copied, 1)

            def copy_z(p, b, h, j):
                act.wait_ge(z_ready, z_count(p, b, h, j))
                wait(act, o_ready, o_count(p, b, j) - 2)
                nc.scalar.activation(z_hi[h][j][:], ps_z[:, :], ACT.Copy).then_inc(z_copied, 1)

            def copy_others(p, events):
                for kind, arg in events:
                    if kind == "z":
                        b, h, j = arg
                        copy_z(p if b >= 0 else p - 1, b % 2, h, j)
                    if kind == "proj":
                        copy_proj(p, arg, 2 * p + 1 + arg // 9, 1 - arg // 9)

            for k in range(9):
                copy_proj(-1, 9 + k, 0, 0)
            for n in range(AHEAD - 1):
                exp(0, n)

            def iteration(p, first, last):
                plan = slot_plan(first, last)
                for s in range(2 * UPH):
                    copy_others(p, plan[s - 1])
                    copy_probs(p, s)
                    n = s + AHEAD - 1
                    if n < 2 * UPH:
                        exp(p, n)
                    elif not last:
                        exp(p + 1, n - 2 * UPH)

            iteration(0, True, False)
            with act.Fori(1, PAIRS - 1) as p:
                iteration(p, False, False)
            iteration(PAIRS - 1, False, True)
            for s in range(2 * UPH - 1, 3 * UPH):
                copy_others(PAIRS - 1, slot_plan(False, True)[s])

        @block.vector
        def _(dve):
            order = [0]

            def then(ins):
                order[0] += 1
                ins.then_inc(dve_order, 1)
                dve.wait_ge(dve_order, order[0])

            dve.wait_ge(x_in, 16)
            for t in range(TT):
                ins = nc.vector.bn_stats(stats[:, t, :], x_tok[:, t, :])
            then(ins)
            for t in range(TT):
                ins = nc.vector.bn_aggr(meanvar[:, t, :], stats[:, t, :])
            ins.then_inc(var_done, 1)
            dve.wait_ge(std_done, 1)
            then(nc.vector.reciprocal(rstd[:], std[:]))
            for t in range(TT):
                nc.vector.tensor_scalar(xn[:, t, :], x_tok[:, t, :], meanvar[:, t, 0:1], rstd[:, t:t + 1],
                                        ALU.subtract, ALU.mult).then_inc(xn_done, 1)
            for g in range(TB):
                dve.wait_ge(xhi_done, g + 1)
                blk = slice(g * BLK, (g + 1) * BLK)
                nc.vector.tensor_tensor(xT_lo[:, blk], xT_bank[g], xT_hi[:, blk].bitcast(F32), ALU.subtract).then_inc(xlo_done, 1)

            def spread(col):
                return col.unsqueeze(2).to_broadcast([P, TT, E])

            dve.wait_ge(logit_ready, 1)
            logits = ps_misc[:, 0:TT * E].rearrange("p (t e) -> p t e", e=E)
            then(nc.vector.reduce_max(top[:, 0, :], logits, AX_X))
            nc.vector.tensor_tensor(logit[:], logits, spread(top[:, 0, :]), ALU.subtract).then_inc(shifted, 1)
            dve.wait_ge(exped, 1)
            dve.wait_ge(const_made, 6)
            now = prob
            for c in range(2):
                then(nc.vector.reduce_max(top[:, c, :], now[:], AX_X))
                then(nc.vector.tensor_tensor(vote[:], now[:], spread(top[:, c, :]), ALU.is_equal))
                then(nc.vector.tensor_tensor(vote[:], vote[:], rank[:], ALU.mult))
                then(nc.vector.reduce_max(top[:, 2, :], vote[:], AX_X))
                then(nc.vector.tensor_tensor(pick[:, c], vote[:], spread(top[:, 2, :]), ALU.is_equal))
                if c == 0:
                    then(nc.vector.scalar_tensor_tensor(out=left[:], in0=pick[:, 0], scalar=-2.0, in1=prob[:],
                                                        op0=ALU.mult, op1=ALU.add))
                    now = left
            then(nc.vector.tensor_tensor(top[:, 3, :], top[:, 0, :], top[:, 1, :], ALU.add))
            then(nc.vector.reciprocal(top[:, 2, :], top[:, 3, :]))
            then(nc.vector.tensor_tensor(vote[:], pick[:, 0], pick[:, 1], ALU.add))
            then(nc.vector.tensor_tensor(left[:], vote[:], prob[:], ALU.mult))
            nc.vector.tensor_tensor(cw[:], left[:], spread(top[:, 2, :]), ALU.mult).then_inc(cw_done, 1)
            nc.vector.memset(y_sc[0][:], 0.0).then_inc(y_scaled, YBUF)

            def experts(it):
                for n in range(UPI + 3):
                    if n < UPI:
                        dve.wait_ge(silu_done, UPI * it + n + 1)
                        dve.wait_ge(up_ready, UPI * it + n + 1)
                        if n >= 2:
                            dve.wait_ge(hidlo_done, UPI * it + n - 1)
                        nc.vector.tensor_tensor(hid[n % 2][:], ps_big[:, n % 2, BLK:2 * BLK], silu[n % 2][:], ALU.mult).then_inc(hid_done, 1)
                    if 1 <= n <= UPI:
                        m = n - 1
                        dve.wait_ge(hidhi_done, UPI * it + m + 1)
                        if m >= 2:
                            dve.wait_ge(down_done, UPI * it + m - 1)
                        nc.vector.tensor_tensor(hid_lo[m % 2][:], hid[m % 2][:], hid_hi[m % 2][:].bitcast(F32), ALU.subtract).then_inc(hidlo_done, 1)
                    if n >= 5 and (n - 5) % 3 == 0:
                        k = (n - 5) // 3
                        if k % TB == 0:
                            dve.wait_ge(cw_in[k // TB], 16 * it + 16)
                        dve.wait_ge(down_done, UPI * it + MT * (k + 1))
                        dve.wait_ge(y_added, BPI * it + k + 1)
                        blk = slice((k % TB) * BLK, (k % TB + 1) * BLK)
                        nc.vector.tensor_tensor(y_sc[k % YBUF][:], ps_mid[:, k % 2, :], cw_bc[k // TB][:, blk], ALU.mult).then_inc(y_scaled, 1)

            with dve.Fori(0, ITER) as it:
                experts(it)

            def row_max(p, n):
                off, width, _ = score_cols(n % QT)
                dve.wait_ge(s_ready, unit_count(p, n))
                nc.vector.tensor_reduce(neg_max[:, n:n + 1], ps_big[:, n % 2, off:off + width], AX_X, ALU.max,
                                        negate=True).then_inc(max_done, 1)

            def recip(p, n):
                dve.wait_ge(exp_done, unit_count(p, n))
                nc.vector.reciprocal(rden[:, n:n + 1], den[:, n:n + 1]).then_inc(rden_done, 1)

            def split_probs(p, n):
                head, i = divmod(n, QT)
                j = i // TPB
                for g in range(GROUPS[i]):
                    count = group_count(p, n) - GROUPS[i] + g + 1
                    tiles = min(TPB, i + 1 - g * TPB)
                    bank = (head * GPH + sum(GROUPS[:i]) + g) % 2
                    dve.wait_ge(pT_copied, count)
                    kt, q = slice(g * TPB, g * TPB + tiles), slice((i % TPB) * P, (i % TPB + 1) * P)
                    nc.vector.tensor_tensor(pT_lo[j][:, kt, q], ps_mid[:, bank, 0:tiles * P].rearrange("p (t q) -> p t q", t=tiles),
                                            pT_hi[j][:, kt, q].bitcast(F32), ALU.subtract).then_inc(pT_split, 1)

            def split_proj(p, k, b_next):
                name = PROJ[k]
                if name[0] == "v":
                    return
                dve.wait_ge(proj_copied, proj_count(p, k))
                if name == "wqkv":
                    nc.vector.scalar_tensor_tensor(out=w_lo[:, 0, :], in0=ps_misc[:, 0:P], scalar=DH ** -0.5,
                                                   in1=w_hi[:, 0, :].bitcast(F32), op0=ALU.mult, op1=ALU.subtract)
                    ins = nc.vector.tensor_tensor(w_lo[:, 1:3, :], ps_misc[:, P:3 * P].rearrange("p (m r) -> p m r", m=2),
                                                  w_hi[:, 1:3, :].bitcast(F32), ALU.subtract)
                elif name == "wo":
                    ins = nc.vector.tensor_tensor(wo_lo[:], ps_misc[:, 0:2 * P].rearrange("p (h d) -> p h d", h=2),
                                                  wo_hi[:].bitcast(F32), ALU.subtract)
                elif name[0] in "qk":
                    c = int(name[1])
                    t = q_parts if name[0] == "q" else k_parts
                    blk = slice(c * BLK, (c + 1) * BLK)
                    ins = nc.vector.tensor_tensor(t[:, 1, blk], ps_misc[:, :], t[:, 0, blk].bitcast(F32), ALU.subtract)
                else:
                    c = int(name[1])
                    tiles = slice(c * TPB, (c + 1) * TPB)
                    ins = nc.vector.tensor_tensor(v_st[b_next][:, tiles, :, 1, :], ps_misc[:, :].rearrange("p (t h c) -> p t h c", t=TPB, h=2),
                                                  v_st[b_next][:, tiles, :, 0, :].bitcast(F32), ALU.subtract)
                ins.then_inc(proj_split, 1)

            def split_z(p, b, h, j):
                dve.wait_ge(z_copied, z_count(p, b, h, j))
                nc.vector.tensor_tensor(z_lo[h][j][:], ps_z[:, :], z_hi[h][j][:].bitcast(F32), ALU.subtract).then_inc(z_split, 1)

            def add_o(p, b, j):
                dve.wait_ge(o_ready, o_count(p, b, j))
                blk = slice(b * S + j * BLK, b * S + (j + 1) * BLK)
                nc.vector.tensor_tensor(acc[:, blk], ps_misc[:, :], acc[:, blk], ALU.add).then_inc(o_added, 1)

            def split_others(p, events):
                for kind, arg in events:
                    if kind == "z":
                        b, h, j = arg
                        split_z(p if b >= 0 else p - 1, b % 2, h, j)
                    if kind == "proj":
                        split_proj(p, arg, 1 - arg // 9)
                    if kind == "o":
                        b, j = arg
                        add_o(p if b >= 0 else p - 1, b % 2, j)

            for k in range(9):
                split_proj(-1, 9 + k, 0)
            dve.wait_ge(y_added, YBUF + E * TB)
            for n in range(AHEAD - 1):
                row_max(0, n)
            recip(0, 0)

            def iteration(p, first, last):
                plan = slot_plan(first, last)
                for s in range(2 * UPH):
                    n = s + AHEAD - 1
                    if n < 2 * UPH:
                        row_max(p, n)
                    elif not last:
                        row_max(p + 1, n - 2 * UPH)
                    n = s + AHEAD - 2
                    if n < 2 * UPH:
                        recip(p, n)
                    elif not last:
                        recip(p + 1, n - 2 * UPH)
                    split_others(p, plan[s - 1])
                    split_probs(p, s)

            iteration(0, True, False)
            with dve.Fori(1, PAIRS - 1) as p:
                iteration(p, False, False)
            iteration(PAIRS - 1, False, True)
            for s in range(2 * UPH - 1, 3 * UPH):
                split_others(PAIRS - 1, slot_plan(False, True)[s])
            for g in range(TB):
                dve.wait_ge(acc_turned, g + 1)
                tiles = slice(g * TPB, (g + 1) * TPB)
                nc.vector.tensor_tensor(x_tok[:, tiles, :], xT_bank[g].rearrange("p (t d) -> p t d", t=TPB),
                                        x_tok[:, tiles, :], ALU.add).then_inc(out_made, 1)

        @block.tensor
        def _(pe):
            def product(dst, w, m, start=True, stop=True):
                nc.tensor.matmul(dst, w[0], m[0], start=start, stop=False, skip_group_check=True)
                nc.tensor.matmul(dst, w[1], m[0], start=False, stop=False, skip_group_check=True)
                return nc.tensor.matmul(dst, w[0], m[1], start=False, stop=stop, skip_group_check=True)

            pe.wait_ge(const_made, 6)
            for t in range(TT):
                pe.wait_ge(xn_done, t + 1)
                ins = nc.tensor.transpose(xT_bank[t // TPB][:, (t % TPB) * P:(t % TPB + 1) * P], xn[:, t, :], ident[:])
                if t % TPB == TPB - 1:
                    ins.then_inc(xT_ready, 1)
            pe.wait_ge(wr_in, 16)
            for t in range(TT):
                pe.wait_ge(xT_copied, t // TPB + 1)
                ins = nc.tensor.matmul(ps_misc[:, t * E:(t + 1) * E], xT[:, t * P:(t + 1) * P], wr_sb[:], start=True, stop=True)
            ins.then_inc(logit_ready, 1)
            pe.wait_ge(cw_done, 1)
            for t in range(TT):
                ins = nc.tensor.transpose(cwT_bank[t // TPB][0:E, (t % TPB) * P:(t % TPB + 1) * P], cw[:, t, :], ident[:])
                if t % TPB == TPB - 1:
                    ins.then_inc(cwT_ready, 1)
            pe.wait_ge(cwT_copied, TB)
            pe.wait_ge(xlo_done, TB)

            def experts(it):
                for n in range(UPI + DOWN_LAG):
                    if n < UPI:
                        j, tb, mt = n // UPE, n % UPE // MT, n % MT
                        if n % UPE == 0:
                            pe.wait_ge(wlo_done, 3 * it + j + 1)
                        if n >= 2:
                            pe.wait_ge(hid_done, UPI * it + n - 1)
                        cols, blk = slice(mt * P, (mt + 1) * P), slice(tb * BLK, (tb + 1) * BLK)
                        xs = (xT_hi[:, blk], xT_lo[:, blk])
                        product(ps_big[:, n % 2, 0:BLK], (g_hi[j][:, cols], g_lo[j][:, cols]), xs).then_inc(gate_ready, 1)
                        product(ps_big[:, n % 2, BLK:2 * BLK], (u_hi[j][:, cols], u_lo[j][:, cols]), xs).then_inc(up_ready, 1)
                    if n >= DOWN_LAG:
                        m = n - DOWN_LAG
                        j, k, mt = m // UPE, m // MT, m % MT
                        pe.wait_ge(hidlo_done, UPI * it + m + 1)
                        if mt == 0:
                            pe.wait_ge(y_scaled, BPI * it + k + 1)
                        ins = product(ps_mid[:, k % 2, :], (d_hi[j][:, mt, :], d_lo[j][:, mt, :]),
                                      (hid_hi[m % 2][:], hid_lo[m % 2][:]), start=mt == 0, stop=mt == MT - 1)
                        ins.then_inc(down_done, 1)

            with pe.Fori(0, ITER) as it:
                experts(it)
            pe.wait_ge(y_added, YBUF + E * TB)

            def scores(p, n):
                half, h, i = n // UPH, n // QT % 2, n % QT
                if n % UPH == 0:
                    pe.wait_ge(stacked, 16 * STACKS * (2 * p + half + 1))
                wait(pe, exp_done, unit_count(p, n) - 2)
                off, width, parts = score_cols(i)
                diag = off + width - P
                w = q_st[half][h][:, i * P:(i + 1) * P]
                for c0, c1 in parts:
                    masked = c0 <= diag < c1
                    if masked:
                        nc.tensor.matmul(ps_big[:, n % 2, diag:diag + P], ident_bf[:], causal_bf[:],
                                         start=True, stop=False, skip_group_check=True)
                    for part in range(2):
                        ins = nc.tensor.matmul(ps_big[:, n % 2, c0:c1], w, k_st[half][h][:, part, c0 - off:c1 - off],
                                               start=part == 0 and not masked, stop=part == 1, skip_group_check=True)
                ins.then_inc(s_ready, 1)

            def turn_probs(p, n):
                head, i = divmod(n, QT)
                pe.wait_ge(normed, unit_count(p, n))
                for g in range(GROUPS[i]):
                    count = group_count(p, n) - GROUPS[i] + g + 1
                    bank = (head * GPH + sum(GROUPS[:i]) + g) % 2
                    wait(pe, pT_split, count - 2)
                    for c in range(min(TPB, i + 1 - g * TPB)):
                        kt = g * TPB + c
                        ins = nc.tensor.transpose(ps_mid[:, bank, c * P:(c + 1) * P], probs[n % 4][:, kt * P:(kt + 1) * P], ident[:])
                    ins.then_inc(t_ready, 1)

            def probs_v(p, b, h, j, k0, k1):
                if k0 == 0:
                    pe.wait_ge(pT_split, group_count(p, b * UPH + h * QT + TPB * (j + 1) - 1))
                    wait(pe, z_split, z_count(p, b, h, j) - 1)
                if k0 == 0 and h == 0 and j == 0:
                    k = 17 if b == 0 else 7
                    pe.wait_ge(proj_split, split_count(p if b else p - 1, k))
                tiles = TPB * (j + 1)
                for kt in range(k0, k1):
                    c0 = min(max(kt - TPB * j, 0), TPB - 2) * P
                    w = v_st[b][:, kt, h, :, :].rearrange("p a c -> p (a c)")
                    nc.tensor.matmul(ps_z[:, c0:BLK], w, pT_hi[j][:, kt, c0:BLK], start=kt == 0, stop=False, skip_group_check=True)
                    ins = nc.tensor.matmul(ps_z[:, c0:BLK], w, pT_lo[j][:, kt, c0:BLK], start=False, stop=kt == tiles - 1, skip_group_check=True)
                if k1 == tiles:
                    ins.then_inc(z_ready, 1)

            last_misc = []

            def misc_free():
                if last_misc:
                    s, value = last_misc.pop()
                    wait(pe, s, value)

            def project(p, k, half_next):
                name = PROJ[k]
                misc_free()
                if name == "wqkv":
                    pe.wait_ge(qkv_in, 48 * (p + 2))
                    for m in range(3):
                        ins = nc.tensor.transpose(ps_misc[:, m * P:(m + 1) * P], raw_qkv[:, m, :], ident[:])
                elif name == "wo":
                    pe.wait_ge(o_in, 32 * (p + 1))
                    for h in range(2):
                        ins = nc.tensor.transpose(ps_misc[:, h * P:(h + 1) * P], raw_o[:, h, :, :].rearrange("d a c -> d (a c)"), ident[:])
                elif name[0] in "qkv":
                    m, c = "qkv".index(name[0]), int(name[1])
                    if name == "q0" and half_next == 0:
                        pe.wait_ge(proj_split, split_count(p, 9))
                    blk = slice(half_next * S + c * BLK, half_next * S + (c + 1) * BLK)
                    ins = product(ps_misc[:, :], (w_hi[:, m, :], w_lo[:, m, :]), (xT_hi[:, blk], xT_lo[:, blk]))
                else:
                    c = int(name[1])
                    if c == 0:
                        pe.wait_ge(proj_copied, proj_count(p, k - 1))
                    for t in range(TPB):
                        kt = c * TPB + t
                        ins = nc.tensor.transpose(ps_misc[:, t * P:(t + 1) * P], vT[:, kt * P:(kt + 1) * P], ident[:])
                ins.then_inc(proj_filled, 1)
                last_misc.append((proj_copied, proj_count(p, k)) if name[0] == "v" else (proj_split, split_count(p, k)))

            def output(p, b, j, previous=False):
                misc_free()
                pe.wait_ge(z_split, z_count(p, b, 1, j))
                if b == 0 and j == 0:
                    pe.wait_ge(proj_split, split_count(p, 8))
                for h in range(2):
                    ins = product(ps_misc[:, :], (wo_hi[:, h, :], wo_lo[:, h, :]), (z_hi[h][j][:], z_lo[h][j][:]),
                                  start=h == 0, stop=h == 1)
                ins.then_inc(o_ready, 1)
                last_misc.append((o_added, o_count(p, b, j)))

            def others(p, events):
                for kind, arg in events:
                    if kind == "pv":
                        b, *rest = arg
                        probs_v(p if b >= 0 else p - 1, b % 2, *rest)
                    if kind == "proj":
                        project(p, arg, 1 - arg // 9)
                    if kind == "o":
                        b, j = arg
                        output(p if b >= 0 else p - 1, b % 2, j)

            for k in range(9):
                project(-1, 9 + k, 0)
            pe.wait_ge(pads_zero, 1)
            for n in range(AHEAD):
                scores(0, n)

            def iteration(p, first, last):
                plan = slot_plan(first, last)
                last_misc[:] = [(proj_split, split_count(-1, 17))] if first else [(o_added, o_count(p - 1, 1, 0))]
                for s in range(2 * UPH):
                    turn_probs(p, s)
                    n = s + AHEAD
                    if n < 2 * UPH:
                        scores(p, n)
                    elif not last:
                        scores(p + 1, n - 2 * UPH)
                    others(p, plan[s])

            iteration(0, True, False)
            with pe.Fori(1, PAIRS - 1) as p:
                iteration(p, False, False)
            iteration(PAIRS - 1, False, True)
            for s in range(2 * UPH, 3 * UPH):
                others(PAIRS - 1, slot_plan(False, True)[s])
            pe.wait_ge(o_added, o_count(PAIRS - 1, 1, QB - 1))
            for t in range(TT):
                ins = nc.tensor.transpose(xT_bank[t // TPB][:, (t % TPB) * P:(t % TPB + 1) * P], acc[:, t * P:(t + 1) * P], ident[:])
                if t % TPB == TPB - 1:
                    ins.then_inc(acc_turned, 1)


_INS = ["L0_attn_x", "L0_attn_W_K", "L0_attn_W_Q", "L0_attn_W_V", "L0_attn_W_O",
        "L0_ffn_Wr", "L0_ffn_Wg", "L0_ffn_Wu", "L0_ffn_Wd"]
_OUTS = [((2, 1024, 128), "float32")]


def kernel(**inputs):
    import numpy as _np
    import concourse.bacc as _bacc
    from concourse import mybir as _mybir
    from concourse.bass_utils import run_bass_kernel_spmd as _run

    nc = _bacc.Bacc("TRN2", target_bir_lowering=False, num_devices=1)
    arrays, args = {}, []
    for name in _INS:
        a = _np.ascontiguousarray(inputs[name])
        arrays[f"in_{name}_dram"] = a
        args.append(nc.dram_tensor(f"in_{name}_dram", a.shape, _mybir.dt.from_np(a.dtype), kind="ExternalInput").ap())
    for i, (shape, dtype) in enumerate(_OUTS):
        dt = _mybir.dt.from_np(_np.dtype(dtype))
        args.append(nc.dram_tensor(f"out_{i}_dram", shape, dt, kind="ExternalOutput").ap())
    bass_layernorm_causal_attention_plus_moe_kernel(nc, *args)
    r = _run(nc, [arrays], core_ids=[0])
    got = tuple(r.results[0][f"out_{i}_dram"] for i in range(len(_OUTS)))
    return got[0]
```

```python
from contextlib import ExitStack

import concourse.bass as bass
from concourse import mybir

ALU = mybir.AluOpType
ACT = mybir.ActivationFunctionType
AX_X = mybir.AxisListType.X
F32 = mybir.dt.float32
F32R = mybir.dt.float32r
BF16 = mybir.dt.bfloat16

P = 128
EPS = 1e-5
MASKED = -1e30


def bass_layernorm_causal_attention_plus_moe_kernel(
    nc: bass.Bass,
    x: bass.AP,
    W_K: bass.AP,
    W_Q: bass.AP,
    W_V: bass.AP,
    W_O: bass.AP,
    Wr: bass.AP,
    Wg: bass.AP,
    Wu: bass.AP,
    Wd: bass.AP,
    out: bass.AP,
):
    BATCH, S, D = x.shape
    HEADS, DH, _ = W_K.shape
    E, _, I = Wg.shape
    T = BATCH * S
    TT = T // P
    QT = S // P
    BLK = 512
    TB = T // BLK
    TPB = BLK // P
    QB = S // BLK
    PAIRS = HEADS // 2
    MT = -(-I // P)
    IP = MT * P
    ILAST = I - (MT - 1) * P
    assert D == P and 2 * DH == P and BATCH == 2 and S == 1024 and MT == 3 and E % 3 == 0

    x_tiles = x.rearrange("b (t p) d -> p (b t) d", p=P)
    out_tiles = out.rearrange("b (t p) d -> p (b t) d", p=P)
    w_pairs = [w.rearrange("(a two) h d -> a (two h) d", two=2) for w in (W_Q, W_K, W_V)]
    cw_dram = nc.dram_tensor("cw_dram", [E, T], F32).ap()

    def wait(eng, sem, value):
        if not isinstance(value, int) or value > 0:
            eng.wait_ge(sem, value)

    with ExitStack() as ctx:
        def sb(name, shape, dt=F32, stack=None):
            return (stack or ctx).enter_context(nc.sbuf_tensor(name, shape, dt))

        def psum(name, shape):
            return ctx.enter_context(nc.psum_tensor(name, shape, F32))

        def sem(name):
            return ctx.enter_context(nc.semaphore(name))

        ps_big = psum("ps_big", [P, 2, 2 * BLK])
        ps_mid = psum("ps_mid", [P, 2, BLK])
        ps_z = psum("ps_z", [P, BLK])
        ps_misc = psum("ps_misc", [P, BLK])

        xT_hi = sb("xT_hi", [P, T], F32R)
        xT_lo = sb("xT_lo", [P, T], F32R)
        acc = sb("acc", [P, T])
        ident = sb("ident", [P, P])
        ident_bf = sb("ident_bf", [P, P], BF16)
        causal_bf = sb("causal_bf", [P, P], BF16)
        eps_col = sb("eps_col", [P, 1])
        unused = sb("unused", [P, 3])
        raw_qkv = sb("raw_qkv", [P, 3, D])
        raw_o = sb("raw_o", [P, P])

        def q_stack(b):
            return [sb(f"q_st{b}{h}", [P, S], F32R) for h in range(2)]

        def k_stack(b):
            return [sb(f"k_st{b}{h}", [P, 2, S], F32R) for h in range(2)]

        def v_stack(b):
            return sb(f"v_st{b}", [P, QT, 2, 2, DH], F32R)

        w_hi = sb("w_hi", [P, 3, P], F32R)
        w_lo = sb("w_lo", [P, 3, P], F32R)
        q_parts = sb("q_parts", [P, 2, S], F32R)
        k_parts = sb("k_parts", [P, 2, S], F32R)
        part_raw = [sb(f"part_raw{j}", [P, BLK]) for j in range(2)]
        vT = sb("vT", [P, S])
        result = q_parts[:].bitcast(F32).rearrange("p a (t d) -> p (a t) d", d=D)
        q_st, k_st, v_st = [q_stack(0)], [k_stack(0)], [v_stack(0)]

        neg_max = sb("neg_max", [P, 4 * QT])
        den = sb("den", [P, 4 * QT])
        rden = sb("rden", [P, 4 * QT])

        moe = ExitStack()
        x_tok = sb("x_tok", [P, TT, D], stack=moe)
        stats = sb("stats", [P, TT, 6], stack=moe)
        meanvar = sb("meanvar", [P, TT, 2], stack=moe)
        std = sb("std", [P, TT], stack=moe)
        rstd = sb("rstd", [P, TT], stack=moe)
        xn = sb("xn", [P, TT, D], stack=moe)
        xT = sb("xT", [P, T], stack=moe)
        wr_sb = sb("wr_sb", [P, E], stack=moe)
        rank = sb("rank", [P, TT, E], stack=moe)
        logit = sb("logit", [P, TT, E], stack=moe)
        prob = sb("prob", [P, TT, E], stack=moe)
        left = sb("left", [P, TT, E], stack=moe)
        pick = sb("pick", [P, 2, TT, E], stack=moe)
        vote = sb("vote", [P, TT, E], stack=moe)
        top = sb("top", [P, 4, TT], stack=moe)
        cw = sb("cw", [P, TT, E], stack=moe)
        cwT = sb("cwT", [E, T], stack=moe)
        raw_g = [sb(f"raw_g{j}", [P, I], stack=moe) for j in range(3)]
        raw_u = [sb(f"raw_u{j}", [P, I], stack=moe) for j in range(3)]
        raw_d = [sb(f"raw_d{j}", [P, MT, D], stack=moe) for j in range(3)]
        g_hi = [sb(f"g_hi{j}", [P, IP], F32R, moe) for j in range(3)]
        g_lo = [sb(f"g_lo{j}", [P, IP], F32R, moe) for j in range(3)]
        u_hi = [sb(f"u_hi{j}", [P, IP], F32R, moe) for j in range(3)]
        u_lo = [sb(f"u_lo{j}", [P, IP], F32R, moe) for j in range(3)]
        d_hi = [sb(f"d_hi{j}", [P, MT, D], F32R, moe) for j in range(3)]
        d_lo = [sb(f"d_lo{j}", [P, MT, D], F32R, moe) for j in range(3)]
        cw_bc = [sb(f"cw_bc{j}", [P, T], stack=moe) for j in range(3)]
        silu = [sb(f"silu{j}", [P, BLK], stack=moe) for j in range(2)]
        hid = [sb(f"hid{j}", [P, BLK], stack=moe) for j in range(2)]
        hid_hi = [sb(f"hid_hi{j}", [P, BLK], F32R, moe) for j in range(2)]
        hid_lo = [sb(f"hid_lo{j}", [P, BLK], F32R, moe) for j in range(2)]
        y_sc = [sb(f"y_sc{j}", [P, BLK], stack=moe) for j in range(2)]
        moe.close()

        wo_hi = sb("wo_hi", [P, D], F32R)
        wo_lo = sb("wo_lo", [P, D], F32R)
        q_st.append(q_stack(1))
        k_st.append(k_stack(1))
        v_st.append(v_stack(1))
        probs = [sb(f"probs{j}", [P, S]) for j in range(4)]
        PT_BUFS = [1, 1]
        pT_hi = [[sb(f"pT_hi{j}{c}", [P, TPB * (j + 1), BLK], F32R) for c in range(PT_BUFS[j])] for j in range(QB)]
        pT_lo = [[sb(f"pT_lo{j}{c}", [P, TPB * (j + 1), BLK], F32R) for c in range(PT_BUFS[j])] for j in range(QB)]
        z_sum = [sb(f"z_sum{j}", [P, BLK]) for j in range(QB)]
        z_hi = [sb(f"z_hi{j}", [P, BLK], F32R) for j in range(QB)]
        z_lo = [sb(f"z_lo{j}", [P, BLK], F32R) for j in range(QB)]

        x_in = [sem(f"x_in{g}") for g in range(TB)]; x_again = sem("x_again")
        wr_in = sem("wr_in"); qkv_in = sem("qkv_in"); o_in = sem("o_in")
        raw_in = [sem(f"raw_in{j}") for j in range(3)]
        cw_in = [sem(f"cw_in{j}") for j in range(3)]
        cw_out = sem("cw_out"); out_sent = sem("out_sent")
        const_made = sem("const_made"); pool_order = sem("pool_order"); dve_order = sem("dve_order")
        var_done = sem("var_done"); std_done = sem("std_done"); xn_done = sem("xn_done")
        xT_ready = sem("xT_ready"); xT_copied = sem("xT_copied"); xhi_done = sem("xhi_done"); xlo_done = sem("xlo_done")
        logit_ready = sem("logit_ready"); shifted = sem("shifted"); exped = sem("exped")
        cw_done = sem("cw_done"); cwT_ready = sem("cwT_ready"); cwT_copied = sem("cwT_copied")
        whi_done = sem("whi_done"); wlo_done = sem("wlo_done")
        gate_ready = sem("gate_ready"); up_ready = sem("up_ready"); silu_done = sem("silu_done")
        hid_done = sem("hid_done"); hidhi_done = sem("hidhi_done"); hidlo_done = sem("hidlo_done")
        down_done = sem("down_done"); y_scaled = sem("y_scaled"); y_added = sem("y_added")
        pads_zero = sem("pads_zero")
        proj_filled = sem("proj_filled"); proj_copied = sem("proj_copied"); proj_split = sem("proj_split")
        part_rounded = sem("part_rounded"); pool_split = sem("pool_split")
        stacked = sem("stacked")
        s_ready = sem("s_ready"); max_done = sem("max_done"); exp_done = sem("exp_done")
        rden_done = sem("rden_done"); normed = sem("normed")
        t_ready = sem("t_ready"); pT_copied = sem("pT_copied"); pT_split = sem("pT_split")
        z_ready = sem("z_ready"); z_moved = sem("z_moved"); z_summed = sem("z_summed")
        zhi_done = sem("zhi_done"); zlo_done = sem("zlo_done")
        o_ready = sem("o_ready"); o_added = sem("o_added")
        acc_turned = sem("acc_turned"); out_made = sem("out_made")

        cwT_bank = [ps_mid[:, 1, :], ps_misc[:, :]] * 2
        xT_bank = [ps_big[:, g // 2, (g % 2) * BLK:(g % 2 + 1) * BLK] for g in range(TB)]

        UPE = TB * MT
        UPI = 3 * UPE
        BPI = 3 * TB
        ITER = E // 3
        YBUF = 2
        DOWN_LAG = 2

        UPH = 2 * QT
        AHEAD = 3
        ORDER = [0, 1, 2, 3, 4, 5, 7, 6]
        GROUPS = [t // TPB + 1 for t in ORDER]
        GPH = sum(GROUPS)
        PROJ = ["q0", "q1", "k0", "k1", "v0", "v1", "t0", "t1", "wo",
                "wqkv", "q0", "q1", "k0", "k1", "v0", "v1", "t0", "t1"]
        PROJ_FIRST = PROJ[9:]
        FIRST_BANK = {"wqkv": ps_z[:, :], "q0": xT_bank[0], "q1": xT_bank[1], "k0": xT_bank[2], "k1": xT_bank[3],
                      "v0": ps_z[:, :], "v1": ps_mid[:, 0, :], "t0": ps_z[:, :], "t1": ps_mid[:, 0, :]}
        PROJ_SLOT = {"wqkv": 1, "q0": 2, "q1": 3, "k0": 4, "k1": 6, "v0": 7, "v1": 9, "t0": 11, "t1": 12, "wo": 14}
        PV_SLOTS = [[(5, 0, 4)], [(8, 0, 3), (9, 3, 4), (10, 4, 8)]]
        SUM_SLOT = [UPH - 2, UPH + 3]
        OUT_SLOT = [UPH, UPH + 5]
        BLOCKS = [0, 1]
        TURNS = [(b, j) for b in range(BATCH) for j in BLOCKS]
        TURN_LAG = [2, 1]
        POOLED = "k"
        SPLIT = [n for n in PROJ if n[0] not in "v" + POOLED]
        assert max(PROJ_SLOT.values()) < UPH <= min(OUT_SLOT)
        SPLIT_FIRST = sum(n[0] not in "v" + POOLED for n in PROJ_FIRST)
        STACKS = 8

        def proj_count(p, k):
            return len(PROJ_FIRST) + len(PROJ) * p + k + 1

        def split_count(p, k):
            return SPLIT_FIRST + len(SPLIT) * p + sum(n[0] not in "v" + POOLED for n in PROJ[:k + 1])

        def pooled_count(p, k):
            return 2 * len(POOLED) * (2 * p + 1) + sum(n[0] in POOLED for n in PROJ[:k + 1])

        def part_done(p, k):
            return (pool_split, pooled_count(p, k)) if PROJ[k][0] in POOLED else (proj_split, split_count(p, k))

        def bank_read(p, k):
            return (proj_copied, proj_count(p, k)) if PROJ[k][0] in "v" + POOLED else (proj_split, split_count(p, k))

        def slot_plan(first, last):
            plan = {s: [] for s in range(-1, 3 * UPH)}
            for b in (-1, 0, 1):
                events = [(PROJ_SLOT[PROJ[k]], ("proj", k)) for k in range(9 * b, 9 * b + 9) if b >= 0 and not (last and b == 1)]
                for j in BLOCKS:
                    for h in range(2):
                        for at, k0, k1 in PV_SLOTS[j]:
                            events.append((h * QT + at, ("pv", (b, h, j, k0, k1))))
                        events.append((h * QT + at, ("z", (b, h, j))))
                    events.append((SUM_SLOT[j], ("zz", (b, j))))
                    events.append((OUT_SLOT[j], ("o", (b, j))))
                    if last and b >= 0:
                        events.append((OUT_SLOT[j] + TURN_LAG[b], ("turn", (b, j))))
                for at, event in events:
                    if at + b * UPH >= -1 and not (b < 0 and first):
                        plan[at + b * UPH].append(event)
            return plan

        def z_count(p, b, h, j):
            return 8 * p + 4 * b + 2 * h + BLOCKS.index(j) + 1

        def o_count(p, b, j):
            return 4 * p + 2 * b + BLOCKS.index(j) + 1

        def turn_count(b, j):
            return TURNS.index((b, j)) + 1

        def part_views(name):
            c = int(name[1])
            t = q_parts if name[0] == "q" else k_parts
            blk = slice(c * BLK, (c + 1) * BLK)
            return part_raw[c][:], t[:, 0, blk], t[:, 1, blk]

        def unit_count(p, n):
            return 2 * UPH * p + n + 1

        def group_count(p, n):
            head, u = divmod(n, QT)
            return 4 * GPH * p + head * GPH + sum(GROUPS[:u + 1])

        def group_bank(n, g):
            head, u = divmod(n, QT)
            return (head * GPH + sum(GROUPS[:u]) + g) % 2

        def last_unit(j):
            return max(u for u in range(QT) if ORDER[u] // TPB == j)

        def score_cols(i):
            width = (i + 1) * P
            off = P if width == BLK + P else 0
            end = max(off + width, 2 * P)
            parts = [(off, min(end, BLK))] + ([(BLK, end)] if end > BLK else [])
            return off, width, parts

        block = ctx.enter_context(nc.Block())

        @block.sync
        def _(sp):
            for g in range(TB):
                tiles = slice(g * TPB, (g + 1) * TPB)
                sp.dma_start(x_tok[:, tiles, :], x_tiles[:, tiles, :]).then_inc(x_in[g], 16)
            sp.dma_start(wr_sb[:], Wr).then_inc(wr_in, 16)

            def load_expert(e, j):
                pick_e = (lambda w: w[e]) if isinstance(e, int) else (lambda w: w[bass.ds(e, 1)].rearrange("a r c -> (a r) c"))
                sp.dma_start(raw_g[j][:], pick_e(Wg)).then_inc(raw_in[j], 16)
                sp.dma_start(raw_u[j][:], pick_e(Wu)).then_inc(raw_in[j], 16)
                wd = pick_e(Wd)
                sp.dma_start(raw_d[j][:, 0:MT - 1, :], wd[0:(MT - 1) * P].rearrange("(m r) c -> r m c", r=P)).then_inc(raw_in[j], 16)
                sp.dma_start(raw_d[j][0:ILAST, MT - 1, :], wd[(MT - 1) * P:I]).then_inc(raw_in[j], 16)

            def load_cw(e, j):
                src = cw_dram[e:e + 1, :] if isinstance(e, int) else cw_dram[bass.ds(e, 1), :]
                sp.dma_start(cw_bc[j][:], src.broadcast_to([P, T])).then_inc(cw_in[j], 16)

            def load_qkv(p):
                for m, w in enumerate(w_pairs):
                    src = w[p] if isinstance(p, int) else w[bass.ds(p, 1)].rearrange("a r d -> (a r) d")
                    sp.dma_start(raw_qkv[:, m, :], src).then_inc(qkv_in, 16)

            def load_o(p):
                src = W_O[:, p * P:(p + 1) * P] if isinstance(p, int) else W_O[:, bass.ds(p * P, P)]
                sp.dma_start(raw_o[:], src).then_inc(o_in, 16)

            def stack(p, b):
                k_q1, k_k1 = (1, 3) if b == 1 else (11, 13)
                before = p if b == 1 else p - 1
                wait(sp, *part_done(before, k_q1))
                for h in range(2):
                    rows = slice(DH * h, DH * (h + 1))
                    for part in range(2):
                        sp.dma_start(q_st[b][h][DH * part:DH * (part + 1), :].bitcast(F32),
                                     q_parts[rows, part, :].bitcast(F32)).then_inc(stacked, 16)
                wait(sp, *part_done(before, k_k1))
                for h in range(2):
                    rows = slice(DH * h, DH * (h + 1))
                    for copy in range(2):
                        sp.dma_start(k_st[b][h][DH * copy:DH * (copy + 1), :, :].bitcast(F32),
                                     k_parts[rows, :, :].bitcast(F32)).then_inc(stacked, 16)

            load_qkv(0)
            for e in range(3):
                load_expert(e, e)
            load_o(0)
            sp.wait_ge(cwT_copied, TB)
            sp.dma_start(cw_dram, cwT[:]).then_inc(cw_out, 16)
            sp.wait_ge(cw_out, 16)
            for e in range(3):
                load_cw(e, e)
            stack(0, 0)
            with sp.Fori(0, ITER - 1) as it:
                for j in range(3):
                    nxt = sp.snap(3 * it + j + 3)
                    sp.wait_ge(wlo_done, 3 * it + j + 1)
                    load_expert(nxt, j)
                    sp.wait_ge(y_scaled, YBUF + 12 * it + 4 * (j + 1))
                    load_cw(nxt, j)

            def iteration(p, last):
                if not last:
                    wait(sp, proj_filled, proj_count(p - 1, 9))
                    load_qkv(p + 1)
                stack(p, 1)
                if not last:
                    wait(sp, proj_filled, proj_count(p, 8))
                    load_o(p + 1)
                    stack(p + 1, 0)

            iteration(0, False)
            with sp.Fori(1, PAIRS - 1) as p:
                iteration(p, False)
            iteration(PAIRS - 1, True)
            sp.wait_ge(stacked, 16 * STACKS * 2 * PAIRS)
            sp.dma_start(result, x_tiles).then_inc(x_again, 16)
            for b, j in TURNS:
                sp.wait_ge(out_made, turn_count(b, j))
                g = QB * b + j
                sp.dma_start(out_tiles[:, g * TPB:(g + 1) * TPB, :], result[:, g * TPB:(g + 1) * TPB, :]).then_inc(out_sent, 16)
            sp.wait_ge(out_sent, 16 * TB)

        @block.gpsimd
        def _(pool):
            pool.memset(ident[:], 0.0).then_inc(pool_order, 1)
            pool.memset(ident_bf[:], 0.0).then_inc(pool_order, 1)
            pool.memset(causal_bf[:], 0.0).then_inc(pool_order, 1)
            pool.memset(rank[:], 0.0).then_inc(pool_order, 1)
            pool.memset(eps_col[:], EPS).then_inc(const_made, 1)
            pool.wait_ge(pool_order, 4)
            pool.affine_select(out=ident[:], in_=ident[:], compare_op=ALU.not_equal, fill=1.0, base=0,
                               pattern=[[-1, P]], channel_multiplier=1).then_inc(const_made, 1)
            pool.affine_select(out=ident_bf[:], in_=ident_bf[:], compare_op=ALU.not_equal, fill=1.0, base=0,
                               pattern=[[-1, P]], channel_multiplier=1).then_inc(const_made, 1)
            pool.affine_select(out=causal_bf[:], in_=causal_bf[:], compare_op=ALU.is_ge, fill=MASKED, base=0,
                               pattern=[[-1, P]], channel_multiplier=1).then_inc(const_made, 1)
            for e in range(E):
                last = pool.memset(rank[:, :, e], float(E - e))
            last.then_inc(const_made, 1)
            for j in range(3):
                for w in (g_hi, g_lo, u_hi, u_lo):
                    pool.memset(w[j][:, I:IP].bitcast(F32), 0.0)
                for w in (d_hi, d_lo):
                    last = pool.memset(w[j][:, MT - 1, :].bitcast(F32), 0.0)
            last.then_inc(const_made, 1)
            pool.memset(acc[:], 0.0).then_inc(y_added, YBUF)

            def split_expert(e, j):
                pool.wait_ge(whi_done, 4 * e + 4)
                pool.tensor_tensor(g_lo[j][:, 0:I], raw_g[j][:], g_hi[j][:, 0:I].bitcast(F32), ALU.subtract)
                pool.tensor_tensor(u_lo[j][:, 0:I], raw_u[j][:], u_hi[j][:, 0:I].bitcast(F32), ALU.subtract)
                pool.tensor_tensor(d_lo[j][:, 0:MT - 1, :], raw_d[j][:, 0:MT - 1, :], d_hi[j][:, 0:MT - 1, :].bitcast(F32), ALU.subtract)
                pool.tensor_tensor(d_lo[j][0:ILAST, MT - 1, :], raw_d[j][0:ILAST, MT - 1, :],
                                   d_hi[j][0:ILAST, MT - 1, :].bitcast(F32), ALU.subtract).then_inc(wlo_done, 1)

            for g in range(TB):
                pool.wait_ge(xhi_done, g + 1)
                blk = slice(g * BLK, (g + 1) * BLK)
                pool.tensor_tensor(xT_lo[:, blk], xT[:, blk], xT_hi[:, blk].bitcast(F32), ALU.subtract).then_inc(xlo_done, 1)

            def split_part(p, k):
                if PROJ[k][0] not in POOLED:
                    return
                pool.wait_ge(part_rounded, pooled_count(p, k))
                raw, hi, lo = part_views(PROJ[k])
                pool.tensor_tensor(lo, raw, hi.bitcast(F32), ALU.subtract).then_inc(pool_split, 1)

            split_expert(0, 0)
            for k in range(9):
                split_part(-1, 9 + k)

            def experts(it, last):
                for k in range(BPI):
                    pool.wait_ge(y_scaled, YBUF + BPI * it + k + 1)
                    blk = slice((k % TB) * BLK, (k % TB + 1) * BLK)
                    pool.tensor_tensor(acc[:, blk], acc[:, blk], y_sc[k % YBUF][:], ALU.add).then_inc(y_added, 1)
                    if k % TB == 1 and not (last and k // TB == 2):
                        split_expert(3 * it + k // TB + 1, (k // TB + 1) % 3)

            with pool.Fori(0, ITER - 1) as it:
                experts(it, False)
            experts(ITER - 1, True)

            pool.wait_ge(y_added, YBUF + E * TB)
            for j in range(QB):
                for t in pT_hi[j] + pT_lo[j]:
                    last = pool.memset(t[:, TPB * (j + 1) - 1, 2 * P:3 * P].bitcast(F32), 0.0)
            last.then_inc(pads_zero, 1)

            def norm(p, n):
                width = (ORDER[n % QT] + 1) * P
                rows = probs[n % 4][:, 0:width]
                col = rden[:, n:n + 1]
                pool.wait_ge(rden_done, unit_count(p, n))
                pool.tensor_tensor(rows, rows, col.to_broadcast([P, width]), ALU.mult).then_inc(normed, 1)

            def split_z(p, b, j):
                pool.wait_ge(zhi_done, o_count(p, b, j))
                pool.tensor_tensor(z_lo[j][:], z_sum[j][:], z_hi[j][:].bitcast(F32), ALU.subtract).then_inc(zlo_done, 1)

            def split_others(p, events):
                for kind, arg in events:
                    if kind == "proj":
                        split_part(p, arg)
                    if kind == "zz":
                        b, j = arg
                        split_z(p if b >= 0 else p - 1, b % 2, j)

            norm(0, 0)

            def iteration(p, first, last):
                plan = slot_plan(first, last)
                for s in range(2 * UPH):
                    n = s + AHEAD - 2
                    if n < 2 * UPH:
                        norm(p, n)
                    elif not last:
                        norm(p + 1, n - 2 * UPH)
                    split_others(p, plan[s - 1])

            iteration(0, True, False)
            with pool.Fori(1, PAIRS - 1) as p:
                iteration(p, False, False)
            iteration(PAIRS - 1, False, True)
            for s in range(2 * UPH - 1, 3 * UPH):
                split_others(PAIRS - 1, slot_plan(False, True)[s])

        @block.scalar
        def _(act):
            def split_expert(e, j, count):
                act.wait_ge(raw_in[j], 64 * count)
                nc.scalar.activation(g_hi[j][:, 0:I], raw_g[j][:], ACT.Copy).then_inc(whi_done, 1)
                nc.scalar.activation(u_hi[j][:, 0:I], raw_u[j][:], ACT.Copy).then_inc(whi_done, 1)
                nc.scalar.activation(d_hi[j][:, 0:MT - 1, :], raw_d[j][:, 0:MT - 1, :], ACT.Copy).then_inc(whi_done, 1)
                nc.scalar.activation(d_hi[j][0:ILAST, MT - 1, :], raw_d[j][0:ILAST, MT - 1, :], ACT.Copy).then_inc(whi_done, 1)

            def copy_proj(p, k, half, b_next, bank=ps_misc[:, :]):
                name = PROJ[k]
                act.wait_ge(proj_filled, proj_count(p, k))
                if name == "q0":
                    wait(act, stacked, 16 * STACKS * half)
                if name == "wqkv":
                    nc.scalar.activation(w_hi[:, 0, :], bank[:, 0:P], ACT.Copy, scale=DH ** -0.5)
                    ins = nc.scalar.activation(w_hi[:, 1:3, :], bank[:, P:3 * P].rearrange("p (m r) -> p m r", m=2), ACT.Copy)
                elif name == "wo":
                    ins = nc.scalar.activation(wo_hi[:], bank[:, 0:P], ACT.Copy)
                elif name[0] in POOLED:
                    c = int(name[1])
                    wait(act, pool_split, pooled_count(p, k) - 2)
                    ins = nc.scalar.activation(part_raw[c][:], bank, ACT.Copy)
                elif name[0] in "qk":
                    c = int(name[1])
                    dst = q_parts if name[0] == "q" else k_parts
                    ins = nc.scalar.activation(dst[:, 0, c * BLK:(c + 1) * BLK], bank, ACT.Copy)
                elif name[0] == "v":
                    c = int(name[1])
                    ins = nc.scalar.activation(vT[:, c * BLK:(c + 1) * BLK], bank, ACT.Copy)
                else:
                    c = int(name[1])
                    ins = nc.scalar.activation(v_st[b_next][:, c * TPB:(c + 1) * TPB, :, 0, :],
                                               bank.rearrange("p (t h c) -> p t h c", t=TPB, h=2), ACT.Copy)
                ins.then_inc(proj_copied, 1)

            def preload(func, c):
                nc.scalar.activation(unused[:, c:c + 1], eps_col[:], func)

            act.wait_ge(const_made, 6)
            preload(ACT.Sqrt, 0)
            for g in range(TB + 2):
                if g < TB:
                    act.wait_ge(var_done, g + 1)
                    tiles = slice(g * TPB, (g + 1) * TPB)
                    nc.scalar.activation(std[:, tiles], meanvar[:, tiles, 1], ACT.Sqrt, bias=eps_col[:]).then_inc(std_done, 1)
                if g >= 2:
                    act.wait_ge(xT_ready, g - 1)
                    blk = slice((g - 2) * BLK, (g - 1) * BLK)
                    nc.scalar.activation(xT[:, blk], xT_bank[g - 2], ACT.Copy).then_inc(xT_copied, 1)
                    nc.scalar.activation(xT_hi[:, blk], xT_bank[g - 2], ACT.Copy).then_inc(xhi_done, 1)
            copy_proj(-1, 9, 0, 0, FIRST_BANK["wqkv"])
            split_expert(0, 0, 1)
            act.wait_ge(shifted, 1)
            nc.scalar.activation(prob[:], logit[:], ACT.Exp).then_inc(exped, 1)

            for k in range(1, 9):
                copy_proj(-1, 9 + k, 0, 0, FIRST_BANK[PROJ_FIRST[k]])
            for g in range(TB):
                act.wait_ge(cwT_ready, g + 1)
                nc.scalar.activation(cwT[:, g * BLK:(g + 1) * BLK], cwT_bank[g][0:E, :], ACT.Copy).then_inc(cwT_copied, 1)

            preload(ACT.Silu, 1)

            def experts(it, last):
                for n in range(UPI + 1):
                    if n < UPI:
                        act.wait_ge(gate_ready, UPI * it + n + 1)
                        if n >= 2:
                            act.wait_ge(hid_done, UPI * it + n - 1)
                        nc.scalar.activation(silu[n % 2][:], ps_big[:, n % 2, 0:BLK], ACT.Silu).then_inc(silu_done, 1)
                    if n >= 1:
                        m = n - 1
                        act.wait_ge(hid_done, UPI * it + m + 1)
                        if m >= 2:
                            act.wait_ge(down_done, UPI * it + m - 1)
                        nc.scalar.activation(hid_hi[m % 2][:], hid[m % 2][:], ACT.Copy).then_inc(hidhi_done, 1)
                    if n % UPE == UPE // 2 and not (last and n // UPE == 2):
                        j = n // UPE
                        split_expert(3 * it + j + 1, (j + 1) % 3, it + 1 + (j + 1) // 3)

            with act.Fori(0, ITER - 1) as it:
                experts(it, False)
            experts(ITER - 1, True)

            def exp(p, n):
                off, width, _ = score_cols(ORDER[n % QT])
                act.wait_ge(max_done, unit_count(p, n))
                if n >= 4:
                    act.wait_ge(t_ready, group_count(p, n - 4))
                else:
                    wait(act, t_ready, group_count(p - 1, n - 4 + 2 * UPH))
                nc.scalar.activation(probs[n % 4][:, 0:width], ps_big[:, n % 2, off:off + width], ACT.Exp,
                                     bias=neg_max[:, n:n + 1], accum_out=den[:, n:n + 1]).then_inc(exp_done, 1)

            def copy_probs(p, n):
                head, i = n // QT, ORDER[n % QT]
                j = i // TPB
                buf = head % PT_BUFS[j]
                if not any(ORDER[u] // TPB == j for u in range(n % QT)):
                    wait(act, z_ready, z_count(p, head // 2, head % 2, j) - 2 * PT_BUFS[j])
                for g in range(i // TPB + 1):
                    count = group_count(p, n) - i // TPB + g
                    tiles = min(TPB, i + 1 - g * TPB)
                    bank = group_bank(n, g)
                    act.wait_ge(t_ready, count)
                    nc.scalar.activation(pT_hi[j][buf][:, g * TPB:g * TPB + tiles, (i % TPB) * P:(i % TPB + 1) * P],
                                         ps_mid[:, bank, 0:tiles * P].rearrange("p (t q) -> p t q", t=tiles),
                                         ACT.Copy).then_inc(pT_copied, 1)

            def move_z(p, b, h, j):
                act.wait_ge(z_ready, z_count(p, b, h, j))
                other = slice(DH * (1 - h), DH * (2 - h))
                wait(act, zlo_done, o_count(p, b, j) - 2)
                nc.scalar.activation(z_sum[j][DH * h:DH * (h + 1), :], ps_z[other, :], ACT.Copy).then_inc(z_moved, 1)

            def copy_z(p, b, j):
                act.wait_ge(z_summed, z_count(p, b, 1, j))
                wait(act, o_ready, o_count(p, b, j) - 2)
                nc.scalar.activation(z_hi[j][:], z_sum[j][:], ACT.Copy).then_inc(zhi_done, 1)

            def copy_others(p, events):
                for kind, arg in events:
                    if kind == "z":
                        b, h, j = arg
                        move_z(p if b >= 0 else p - 1, b % 2, h, j)
                    if kind == "zz":
                        b, j = arg
                        copy_z(p if b >= 0 else p - 1, b % 2, j)
                    if kind == "proj":
                        copy_proj(p, arg, 2 * p + 1 + arg // 9, 1 - arg // 9)

            preload(ACT.Exp, 2)
            act.wait_ge(y_added, YBUF + E * TB)
            for n in range(AHEAD - 1):
                exp(0, n)

            def iteration(p, first, last):
                plan = slot_plan(first, last)
                for s in range(2 * UPH):
                    copy_others(p, plan[s - 1])
                    copy_probs(p, s)
                    n = s + AHEAD - 1
                    if n < 2 * UPH:
                        exp(p, n)
                    elif not last:
                        exp(p + 1, n - 2 * UPH)

            iteration(0, True, False)
            with act.Fori(1, PAIRS - 1) as p:
                iteration(p, False, False)
            iteration(PAIRS - 1, False, True)
            for s in range(2 * UPH - 1, 3 * UPH):
                copy_others(PAIRS - 1, slot_plan(False, True)[s])

        @block.vector
        def _(dve):
            order = [0]

            def then(ins):
                order[0] += 1
                ins.then_inc(dve_order, 1)
                dve.wait_ge(dve_order, order[0])

            def split_proj(p, k, b_next, bank=ps_misc[:, :]):
                name = PROJ[k]
                if name[0] == "v":
                    return
                dve.wait_ge(proj_copied, proj_count(p, k))
                if name[0] in POOLED:
                    raw, hi, _ = part_views(name)
                    nc.vector.tensor_copy(hi, raw).then_inc(part_rounded, 1)
                    return
                if name == "wqkv":
                    nc.vector.scalar_tensor_tensor(out=w_lo[:, 0, :], in0=bank[:, 0:P], scalar=DH ** -0.5,
                                                   in1=w_hi[:, 0, :].bitcast(F32), op0=ALU.mult, op1=ALU.subtract)
                    ins = nc.vector.tensor_tensor(w_lo[:, 1:3, :], bank[:, P:3 * P].rearrange("p (m r) -> p m r", m=2),
                                                  w_hi[:, 1:3, :].bitcast(F32), ALU.subtract)
                elif name == "wo":
                    ins = nc.vector.tensor_tensor(wo_lo[:], bank[:, 0:P], wo_hi[:].bitcast(F32), ALU.subtract)
                elif name[0] in "qk":
                    c = int(name[1])
                    t = q_parts if name[0] == "q" else k_parts
                    blk = slice(c * BLK, (c + 1) * BLK)
                    ins = nc.vector.tensor_tensor(t[:, 1, blk], bank, t[:, 0, blk].bitcast(F32), ALU.subtract)
                else:
                    c = int(name[1])
                    tiles = slice(c * TPB, (c + 1) * TPB)
                    ins = nc.vector.tensor_tensor(v_st[b_next][:, tiles, :, 1, :], bank.rearrange("p (t h c) -> p t h c", t=TPB, h=2),
                                                  v_st[b_next][:, tiles, :, 0, :].bitcast(F32), ALU.subtract)
                ins.then_inc(proj_split, 1)

            for g in range(TB + 1):
                tiles = range(g * TPB, (g + 1) * TPB)
                if g < TB:
                    dve.wait_ge(x_in[g], 16)
                    for t in tiles:
                        ins = nc.vector.bn_stats(stats[:, t, :], x_tok[:, t, :])
                    then(ins)
                    for t in tiles:
                        ins = nc.vector.bn_aggr(meanvar[:, t, :], stats[:, t, :])
                    ins.then_inc(var_done, 1)
                if g >= 1:
                    dve.wait_ge(std_done, g)
                    then(nc.vector.reciprocal(rstd[:, (g - 1) * TPB:g * TPB], std[:, (g - 1) * TPB:g * TPB]))
                    for t in range((g - 1) * TPB, g * TPB):
                        nc.vector.tensor_scalar(xn[:, t, :], x_tok[:, t, :], meanvar[:, t, 0:1], rstd[:, t:t + 1],
                                                ALU.subtract, ALU.mult).then_inc(xn_done, 1)
            split_proj(-1, 9, 0, FIRST_BANK["wqkv"])

            def spread(col):
                return col.unsqueeze(2).to_broadcast([P, TT, E])

            dve.wait_ge(logit_ready, 1)
            logits = ps_misc[:, 0:TT * E].rearrange("p (t e) -> p t e", e=E)
            then(nc.vector.reduce_max(top[:, 0, :], logits, AX_X))
            nc.vector.tensor_tensor(logit[:], logits, spread(top[:, 0, :]), ALU.subtract).then_inc(shifted, 1)
            dve.wait_ge(shifted, 1)
            dve.wait_ge(const_made, 6)
            now = logit
            for c in range(2):
                if c == 1:
                    then(nc.vector.scalar_tensor_tensor(out=left[:], in0=pick[:, 0], scalar=MASKED, in1=logit[:],
                                                        op0=ALU.mult, op1=ALU.add))
                    then(nc.vector.reduce_max(top[:, 1, :], left[:], AX_X))
                    then(nc.vector.tensor_tensor(left[:], left[:], spread(top[:, 1, :]), ALU.subtract))
                    now = left
                then(nc.vector.scalar_tensor_tensor(out=vote[:], in0=now[:], scalar=0.0, in1=rank[:],
                                                    op0=ALU.is_equal, op1=ALU.mult))
                then(nc.vector.reduce_max(top[:, 2, :], vote[:], AX_X))
                then(nc.vector.tensor_tensor(pick[:, c], vote[:], spread(top[:, 2, :]), ALU.is_equal))
            then(nc.vector.tensor_tensor(vote[:], pick[:, 0], pick[:, 1], ALU.add))
            dve.wait_ge(exped, 1)
            then(nc.vector.tensor_tensor(left[:], vote[:], prob[:], ALU.mult))
            then(nc.vector.tensor_reduce(top[:, 3, :], left[:], AX_X, ALU.add))
            then(nc.vector.reciprocal(top[:, 2, :], top[:, 3, :]))
            nc.vector.tensor_tensor(cw[:], left[:], spread(top[:, 2, :]), ALU.mult).then_inc(cw_done, 1)
            nc.vector.memset(y_sc[0][:], 0.0).then_inc(y_scaled, YBUF)
            for k in range(1, 9):
                split_proj(-1, 9 + k, 0, FIRST_BANK[PROJ_FIRST[k]])

            def experts(it):
                for n in range(UPI + 3):
                    if n < UPI:
                        dve.wait_ge(silu_done, UPI * it + n + 1)
                        dve.wait_ge(up_ready, UPI * it + n + 1)
                        if n >= 2:
                            dve.wait_ge(hidlo_done, UPI * it + n - 1)
                        nc.vector.tensor_tensor(hid[n % 2][:], ps_big[:, n % 2, BLK:2 * BLK], silu[n % 2][:], ALU.mult).then_inc(hid_done, 1)
                    if 1 <= n <= UPI:
                        m = n - 1
                        dve.wait_ge(hidhi_done, UPI * it + m + 1)
                        if m >= 2:
                            dve.wait_ge(down_done, UPI * it + m - 1)
                        nc.vector.tensor_tensor(hid_lo[m % 2][:], hid[m % 2][:], hid_hi[m % 2][:].bitcast(F32), ALU.subtract).then_inc(hidlo_done, 1)
                    if n >= 5 and (n - 5) % 3 == 0:
                        k = (n - 5) // 3
                        if k % TB == 0:
                            dve.wait_ge(cw_in[k // TB], 16 * it + 16)
                        dve.wait_ge(down_done, UPI * it + MT * (k + 1))
                        dve.wait_ge(y_added, BPI * it + k + 1)
                        blk = slice((k % TB) * BLK, (k % TB + 1) * BLK)
                        nc.vector.tensor_tensor(y_sc[k % YBUF][:], ps_mid[:, k % 2, :], cw_bc[k // TB][:, blk], ALU.mult).then_inc(y_scaled, 1)

            with dve.Fori(0, ITER) as it:
                experts(it)

            def row_max(p, n):
                off, width, _ = score_cols(ORDER[n % QT])
                dve.wait_ge(s_ready, unit_count(p, n))
                nc.vector.tensor_reduce(neg_max[:, n:n + 1], ps_big[:, n % 2, off:off + width], AX_X, ALU.max,
                                        negate=True).then_inc(max_done, 1)

            def recip(p, n):
                dve.wait_ge(exp_done, unit_count(p, n))
                nc.vector.reciprocal(rden[:, n:n + 1], den[:, n:n + 1]).then_inc(rden_done, 1)

            def split_probs(p, n):
                head, i = n // QT, ORDER[n % QT]
                j = i // TPB
                buf = head % PT_BUFS[j]
                for g in range(i // TPB + 1):
                    count = group_count(p, n) - i // TPB + g
                    tiles = min(TPB, i + 1 - g * TPB)
                    bank = group_bank(n, g)
                    dve.wait_ge(pT_copied, count)
                    kt, q = slice(g * TPB, g * TPB + tiles), slice((i % TPB) * P, (i % TPB + 1) * P)
                    nc.vector.tensor_tensor(pT_lo[j][buf][:, kt, q], ps_mid[:, bank, 0:tiles * P].rearrange("p (t q) -> p t q", t=tiles),
                                            pT_hi[j][buf][:, kt, q].bitcast(F32), ALU.subtract).then_inc(pT_split, 1)

            def sum_z(p, b, h, j):
                dve.wait_ge(z_moved, z_count(p, b, h, j))
                rows = slice(DH * h, DH * (h + 1))
                nc.vector.tensor_tensor(z_sum[j][rows, :], ps_z[rows, :], z_sum[j][rows, :], ALU.add).then_inc(z_summed, 1)

            def add_o(p, b, j):
                dve.wait_ge(o_ready, o_count(p, b, j))
                blk = slice(b * S + j * BLK, b * S + (j + 1) * BLK)
                nc.vector.tensor_tensor(acc[:, blk], ps_misc[:, :], acc[:, blk], ALU.add).then_inc(o_added, 1)

            def add_x(b, j):
                dve.wait_ge(acc_turned, turn_count(b, j))
                dve.wait_ge(x_again, 16)
                g = QB * b + j
                tiles = slice(g * TPB, (g + 1) * TPB)
                nc.vector.tensor_tensor(result[:, tiles, :], ps_misc[:, :].rearrange("p (t d) -> p t d", t=TPB),
                                        result[:, tiles, :], ALU.add).then_inc(out_made, 1)

            def split_others(p, events):
                for kind, arg in events:
                    if kind == "turn":
                        add_x(*arg)
                    if kind == "z":
                        b, h, j = arg
                        sum_z(p if b >= 0 else p - 1, b % 2, h, j)
                    if kind == "proj":
                        split_proj(p, arg, 1 - arg // 9)
                    if kind == "o":
                        b, j = arg
                        add_o(p if b >= 0 else p - 1, b % 2, j)

            for n in range(AHEAD - 1):
                row_max(0, n)
            recip(0, 0)

            def iteration(p, first, last):
                plan = slot_plan(first, last)
                for s in range(2 * UPH):
                    n = s + AHEAD - 2
                    if n < 2 * UPH:
                        recip(p, n)
                    elif not last:
                        recip(p + 1, n - 2 * UPH)
                    n = s + AHEAD - 1
                    if n < 2 * UPH:
                        row_max(p, n)
                    elif not last:
                        row_max(p + 1, n - 2 * UPH)
                    split_others(p, plan[s - 1])
                    split_probs(p, s)

            iteration(0, True, False)
            with dve.Fori(1, PAIRS - 1) as p:
                iteration(p, False, False)
            iteration(PAIRS - 1, False, True)
            for s in range(2 * UPH - 1, 3 * UPH):
                split_others(PAIRS - 1, slot_plan(False, True)[s])

        @block.tensor
        def _(pe):
            def product(dst, w, m, start=True, stop=True):
                nc.tensor.matmul(dst, w[0], m[0], start=start, stop=False, skip_group_check=True)
                nc.tensor.matmul(dst, w[1], m[0], start=False, stop=False, skip_group_check=True)
                return nc.tensor.matmul(dst, w[0], m[1], start=False, stop=stop, skip_group_check=True)

            def fill_proj(name, half_next, bank=ps_misc[:, :]):
                if name == "wqkv":
                    for m in range(3):
                        ins = nc.tensor.transpose(bank[:, m * P:(m + 1) * P], raw_qkv[:, m, :], ident[:])
                elif name == "wo":
                    ins = nc.tensor.transpose(bank[:, 0:P], raw_o[:], ident[:])
                elif name[0] in "qkv":
                    m, c = "qkv".index(name[0]), int(name[1])
                    blk = slice(half_next * S + c * BLK, half_next * S + (c + 1) * BLK)
                    ins = product(bank, (w_hi[:, m, :], w_lo[:, m, :]), (xT_hi[:, blk], xT_lo[:, blk]))
                else:
                    for t in range(TPB):
                        kt = int(name[1]) * TPB + t
                        ins = nc.tensor.transpose(bank[:, t * P:(t + 1) * P], vT[:, kt * P:(kt + 1) * P], ident[:])
                ins.then_inc(proj_filled, 1)

            pe.wait_ge(const_made, 6)
            for g in range(TB + 1):
                if g < TB:
                    for t in range(TPB):
                        pe.wait_ge(xn_done, g * TPB + t + 1)
                        ins = nc.tensor.transpose(xT_bank[g][:, t * P:(t + 1) * P], xn[:, g * TPB + t, :], ident[:])
                    ins.then_inc(xT_ready, 1)
                if g == TB - 1:
                    pe.wait_ge(qkv_in, 48)
                    fill_proj("wqkv", 0, FIRST_BANK["wqkv"])
                if g == 1:
                    pe.wait_ge(wr_in, 16)
                if g >= 1:
                    pe.wait_ge(xT_copied, g)
                    for t in range((g - 1) * TPB, g * TPB):
                        ins = nc.tensor.matmul(ps_misc[:, t * E:(t + 1) * E], xT[:, t * P:(t + 1) * P], wr_sb[:], start=True, stop=True)
            ins.then_inc(logit_ready, 1)
            pe.wait_ge(proj_split, 1)
            pe.wait_ge(xlo_done, TB)
            pe.wait_ge(xhi_done, TB)
            for name in PROJ_FIRST[1:]:
                if name == "t0":
                    pe.wait_ge(proj_copied, 7)
                fill_proj(name, 0, FIRST_BANK[name])
            pe.wait_ge(cw_done, 1)
            for t in range(TT):
                if t % TPB == 0:
                    wait(pe, cwT_copied, t // TPB - 1)
                ins = nc.tensor.transpose(cwT_bank[t // TPB][0:E, (t % TPB) * P:(t % TPB + 1) * P], cw[:, t, :], ident[:])
                if t % TPB == TPB - 1:
                    ins.then_inc(cwT_ready, 1)
            pe.wait_ge(cwT_copied, TB)
            pe.wait_ge(proj_split, SPLIT_FIRST)
            pe.wait_ge(proj_copied, len(PROJ_FIRST))

            def experts(it):
                for n in range(UPI + DOWN_LAG):
                    if n < UPI:
                        j, tb, mt = n // UPE, n % UPE // MT, n % MT
                        if n % UPE == 0:
                            pe.wait_ge(wlo_done, 3 * it + j + 1)
                        if n >= 2:
                            pe.wait_ge(hid_done, UPI * it + n - 1)
                        cols, blk = slice(mt * P, (mt + 1) * P), slice(tb * BLK, (tb + 1) * BLK)
                        xs = (xT_hi[:, blk], xT_lo[:, blk])
                        product(ps_big[:, n % 2, 0:BLK], (g_hi[j][:, cols], g_lo[j][:, cols]), xs).then_inc(gate_ready, 1)
                        product(ps_big[:, n % 2, BLK:2 * BLK], (u_hi[j][:, cols], u_lo[j][:, cols]), xs).then_inc(up_ready, 1)
                    if n >= DOWN_LAG:
                        m = n - DOWN_LAG
                        j, k, mt = m // UPE, m // MT, m % MT
                        pe.wait_ge(hidlo_done, UPI * it + m + 1)
                        if mt == 0:
                            pe.wait_ge(y_scaled, BPI * it + k + 1)
                        ins = product(ps_mid[:, k % 2, :], (d_hi[j][:, mt, :], d_lo[j][:, mt, :]),
                                      (hid_hi[m % 2][:], hid_lo[m % 2][:]), start=mt == 0, stop=mt == MT - 1)
                        ins.then_inc(down_done, 1)

            with pe.Fori(0, ITER) as it:
                experts(it)
            pe.wait_ge(hid_done, UPI * ITER)

            def scores(p, n):
                half, h, i = n // UPH, n // QT % 2, ORDER[n % QT]
                if n % UPH == 0:
                    pe.wait_ge(stacked, 16 * STACKS * (2 * p + half + 1))
                wait(pe, exp_done, unit_count(p, n) - 2)
                off, width, parts = score_cols(i)
                diag = off + width - P
                w = q_st[half][h][:, i * P:(i + 1) * P]
                for c0, c1 in parts:
                    masked = c0 <= diag < c1
                    if masked:
                        nc.tensor.matmul(ps_big[:, n % 2, diag:diag + P], ident_bf[:], causal_bf[:],
                                         start=True, stop=False, skip_group_check=True)
                    for part in range(2):
                        ins = nc.tensor.matmul(ps_big[:, n % 2, c0:c1], w, k_st[half][h][:, part, c0 - off:c1 - off],
                                               start=part == 0 and not masked, stop=part == 1, skip_group_check=True)
                ins.then_inc(s_ready, 1)

            def turn_probs(p, n):
                i = ORDER[n % QT]
                pe.wait_ge(normed, unit_count(p, n))
                for g in range(i // TPB + 1):
                    count = group_count(p, n) - i // TPB + g
                    bank = group_bank(n, g)
                    wait(pe, pT_split, count - 2)
                    for c in range(min(TPB, i + 1 - g * TPB)):
                        kt = g * TPB + c
                        ins = nc.tensor.transpose(ps_mid[:, bank, c * P:(c + 1) * P], probs[n % 4][:, kt * P:(kt + 1) * P], ident[:])
                    ins.then_inc(t_ready, 1)

            def probs_v(p, b, h, j, k0, k1):
                if k0 == 0:
                    pe.wait_ge(pT_split, group_count(p, b * UPH + h * QT + last_unit(j)))
                    wait(pe, z_summed, z_count(p, b, h, j) - 1)
                if k0 == 0 and h == 0 and j == BLOCKS[0]:
                    k = 17 if b == 0 else 7
                    pe.wait_ge(*part_done(p if b else p - 1, k))
                tiles = TPB * (j + 1)
                buf = (2 * b + h) % PT_BUFS[j]
                for kt in range(k0, k1):
                    c0 = min(max(kt - TPB * j, 0), TPB - 2) * P
                    w = v_st[b][:, kt, h, :, :].rearrange("p a c -> p (a c)")
                    nc.tensor.matmul(ps_z[:, c0:BLK], w, pT_hi[j][buf][:, kt, c0:BLK], start=kt == 0, stop=False, skip_group_check=True)
                    ins = nc.tensor.matmul(ps_z[:, c0:BLK], w, pT_lo[j][buf][:, kt, c0:BLK], start=False, stop=kt == tiles - 1, skip_group_check=True)
                if k1 == tiles:
                    ins.then_inc(z_ready, 1)

            last_misc = []

            def misc_free():
                if last_misc:
                    s, value = last_misc.pop()
                    wait(pe, s, value)

            def project(p, k, half_next):
                name = PROJ[k]
                misc_free()
                if name == "wqkv":
                    pe.wait_ge(qkv_in, 48 * (p + 2))
                elif name == "wo":
                    pe.wait_ge(o_in, 16 * (p + 1))
                elif name == "q0" and half_next == 0:
                    pe.wait_ge(proj_split, split_count(p, 9))
                elif name == "t0":
                    pe.wait_ge(proj_copied, proj_count(p, k - 1))
                fill_proj(name, half_next)
                last_misc.append(bank_read(p, k))

            def output(p, b, j):
                misc_free()
                pe.wait_ge(zlo_done, o_count(p, b, j))
                if b == 0 and j == BLOCKS[0]:
                    pe.wait_ge(proj_split, split_count(p, 8))
                product(ps_misc[:, :], (wo_hi[:], wo_lo[:]), (z_hi[j][:], z_lo[j][:])).then_inc(o_ready, 1)
                last_misc.append((o_added, o_count(p, b, j)))

            def turn_sum(b, j):
                misc_free()
                pe.wait_ge(o_added, o_count(PAIRS - 1, b, j))
                for t in range(TPB):
                    cols = slice(b * S + j * BLK + t * P, b * S + j * BLK + (t + 1) * P)
                    ins = nc.tensor.transpose(ps_misc[:, t * P:(t + 1) * P], acc[:, cols], ident[:])
                ins.then_inc(acc_turned, 1)
                last_misc.append((out_made, turn_count(b, j)))

            def others(p, events):
                for kind, arg in events:
                    if kind == "turn":
                        turn_sum(*arg)
                    if kind == "pv":
                        b, *rest = arg
                        probs_v(p if b >= 0 else p - 1, b % 2, *rest)
                    if kind == "proj":
                        project(p, arg, 1 - arg // 9)
                    if kind == "o":
                        b, j = arg
                        output(p if b >= 0 else p - 1, b % 2, j)

            for n in range(AHEAD):
                scores(0, n)
            pe.wait_ge(pads_zero, 1)

            def iteration(p, first, last):
                plan = slot_plan(first, last)
                last_misc[:] = [bank_read(p - 1, 17)]
                for s in range(2 * UPH):
                    turn_probs(p, s)
                    n = s + AHEAD
                    if n < 2 * UPH:
                        scores(p, n)
                    elif not last:
                        scores(p + 1, n - 2 * UPH)
                    others(p, plan[s])

            iteration(0, True, False)
            with pe.Fori(1, PAIRS - 1) as p:
                iteration(p, False, False)
            iteration(PAIRS - 1, False, True)
            for s in range(2 * UPH, 3 * UPH):
                others(PAIRS - 1, slot_plan(False, True)[s])


_INS = ["L0_attn_x", "L0_attn_W_K", "L0_attn_W_Q", "L0_attn_W_V", "L0_attn_W_O",
        "L0_ffn_Wr", "L0_ffn_Wg", "L0_ffn_Wu", "L0_ffn_Wd"]
_OUTS = [((2, 1024, 128), "float32")]


def kernel(**inputs):
    import numpy as _np
    import concourse.bacc as _bacc
    from concourse import mybir as _mybir
    from concourse.bass_utils import run_bass_kernel_spmd as _run

    nc = _bacc.Bacc("TRN2", target_bir_lowering=False, num_devices=1)
    arrays, args = {}, []
    for name in _INS:
        a = _np.ascontiguousarray(inputs[name])
        arrays[f"in_{name}_dram"] = a
        args.append(nc.dram_tensor(f"in_{name}_dram", a.shape, _mybir.dt.from_np(a.dtype), kind="ExternalInput").ap())
    for i, (shape, dtype) in enumerate(_OUTS):
        dt = _mybir.dt.from_np(_np.dtype(dtype))
        args.append(nc.dram_tensor(f"out_{i}_dram", shape, dt, kind="ExternalOutput").ap())
    bass_layernorm_causal_attention_plus_moe_kernel(nc, *args)
    r = _run(nc, [arrays], core_ids=[0])
    got = tuple(r.results[0][f"out_{i}_dram"] for i in range(len(_OUTS)))
    return got[0]
```
